# Optimizing a Trainium2 kernel written in Bass

```python
import numpy as np
import jax
import jax.numpy as jnp

def _softmax(x, axis=-1):
    return jax.nn.softmax(x, axis=axis)
def _gelu(x):
    return jax.nn.gelu(x, approximate=True)
def _silu(x):
    return jax.nn.silu(x)
def _sigmoid(x):
    return jax.nn.sigmoid(x)
def _layernorm(x, axis=-1, eps=1e-5):
    m = jnp.mean(x, axis=axis, keepdims=True)
    v = jnp.var(x, axis=axis, keepdims=True)
    return (x - m) / jnp.sqrt(v + eps)
def _scatter_add(tgt, idx, src, axis=0):
    return tgt.at[idx].add(src)
def _segment_sum(src, seg, n):
    return jax.ops.segment_sum(src, seg, n)

kernel_name = 'mk_conv_preact_d2_conv_nchw32_21909f'

def setup_inputs(seed: int = 0):
    np.random.seed(seed)
    _w = jnp.asarray
    def _rec_inputs():
        import jax
        import jax.numpy as jnp
        _gk = jax.random.key(seed)
        x = -0.000125 + 0.9999 * jax.random.normal(jax.random.fold_in(_gk, 1), (16, 32, 256, 256), jnp.float32)
        return x
    x = _rec_inputs()
    def _L0_conv_setup():
        import jax, jax.numpy as jnp
        import numpy as np
        MODES1 = 16
        MODES2 = 16
        key = jax.random.key(seed)
        k1, k2, k3 = jax.random.split(key, 3)
        B, Cin, Cout, H, W = (16, 32, 32, 256, 256)
        scale = (1.0 / (Cin * Cout)) ** 0.5
        x = jax.random.normal(k1, (B, Cin, H, W), dtype=jnp.float32)
        w_real = jax.random.normal(k2, (Cin, Cout, MODES1, MODES2), dtype=jnp.float32) * scale
        w_imag = jax.random.normal(k3, (Cin, Cout, MODES1, MODES2), dtype=jnp.float32) * scale
        return {'x': x, 'w_real': w_real, 'w_imag': w_imag}
    _L0_conv_all = _L0_conv_setup()
    _L0_conv_in = {k: v for k, v in _L0_conv_all.items() if k in ('w_real', 'w_imag', )}
    del _L0_conv_all

    def _L1_conv_setup():
        import jax, jax.numpy as jnp
        import numpy as np
        key = jax.random.key(seed)
        k1, k2, k3 = jax.random.split(key, 3)
        x = jax.random.normal(k1, (8, 32, 128, 128), dtype=jnp.float32)
        weight = jax.random.normal(k2, (32, 32, 3, 3), dtype=jnp.float32)
        bias = jax.random.normal(k3, (32,), dtype=jnp.float32)
        return {'x': x, 'weight': weight, 'bias': bias, 'stride': 1, 'padding': 1}
    _L1_conv_all = _L1_conv_setup()
    _L1_conv_in = {k: v for k, v in _L1_conv_all.items() if k in ('weight', 'bias', )}
    del _L1_conv_all

    return {
        "x": x,
        "L0_conv_w_real": _L0_conv_in["w_real"],
        "L0_conv_w_imag": _L0_conv_in["w_imag"],
        "L1_conv_weight": _L1_conv_in["weight"],
        "L1_conv_bias": _L1_conv_in["bias"],
    }

def reference(x, L0_conv_w_real, L0_conv_w_imag, L1_conv_weight, L1_conv_bias):
    import jax
    import jax.numpy as jnp
    def _L0_conv_ref(x, w_real, w_imag):
        import jax, jax.numpy as jnp
        import numpy as np
        MODES1 = 16
        MODES2 = 16
        B, Cin, H, W = x.shape
        Cout = w_real.shape[1]
        m1 = min(MODES1, H)
        m2 = min(MODES2, W)
        weight = w_real + 1j * w_imag
        x_ft = jnp.fft.fft2(x, axes=(-2, -1))
        x_sub = x_ft[:, :, :m1, :m2]
        out_sub = jnp.einsum('bimn,iomn->bomn', x_sub, weight[:, :, :m1, :m2])
        out_ft = jnp.zeros((B, Cout, H, W), dtype=x_ft.dtype)
        out_ft = out_ft.at[:, :, :m1, :m2].add(out_sub)
        return jnp.fft.ifft2(out_ft, axes=(-2, -1)).real

    def _L1_conv_ref(x, weight, bias, stride, padding):
        import jax, jax.numpy as jnp
        import numpy as np
        B, C, H, W = x.shape
        O, _, K, _ = weight.shape
        fft_H = 2 ** int(np.ceil(np.log2(H + K - 1)))
        fft_W = 2 ** int(np.ceil(np.log2(W + K - 1)))
        px = jnp.pad(x, ((0, 0), (0, 0), (0, fft_H - H), (0, fft_W - W)))
        fx = jnp.fft.fft2(px, norm='ortho')
        pw = jnp.pad(weight, ((0, 0), (0, 0), (0, fft_H - K), (0, fft_W - K)))
        wf = jnp.fft.fft2(pw, norm='ortho')
        fout = jnp.einsum('bihw,oihw->bohw', fx, wf)
        sp = jnp.fft.ifft2(fout, norm='ortho').real
        out_h = (H + 2 * padding - K) // stride + 1
        out_w = (W + 2 * padding - K) // stride + 1
        sh = (fft_H - out_h) // 2
        sw = (fft_W - out_w) // 2
        out = sp[:, :, sh:sh + out_h, sw:sw + out_w]
        return out + bias[None, :, None, None]

    def _gn(v, G=16, eps=1e-5):
        B_, C_, H_, W_ = v.shape
        g = v.reshape(B_, G, C_ // G, H_, W_)
        m = jnp.mean(g, axis=(2, 3, 4), keepdims=True)
        s = jnp.var(g, axis=(2, 3, 4), keepdims=True)
        return ((g - m) / jnp.sqrt(s + eps)).reshape(v.shape)

    def _ln_c(v, eps=1e-6):
        m = jnp.mean(v, axis=1, keepdims=True)
        s = jnp.var(v, axis=1, keepdims=True)
        return (v - m) / jnp.sqrt(s + eps)

    def _ln_t(v, eps=1e-5):
        m = jnp.mean(v, axis=-1, keepdims=True)
        s = jnp.var(v, axis=-1, keepdims=True)
        return (v - m) / jnp.sqrt(s + eps)

    def _to_tokens(v):
        B_, C_, H_, W_ = v.shape
        return v.reshape(B_, C_, H_ * W_).transpose(0, 2, 1)
    def _from_tokens(t, like):
        B_, C_, H_, W_ = like.shape
        return t.transpose(0, 2, 1).reshape(B_, C_, H_, W_)

    x = x + _L0_conv_ref(_gn(x), L0_conv_w_real, L0_conv_w_imag)
    x = x + _L1_conv_ref(_gn(x), L1_conv_weight, L1_conv_bias, 1, 1)
    return x


_drawn_inputs = setup_inputs


def setup_inputs(seed=0):
    import zlib

    import numpy as np

    out = dict(_drawn_inputs(seed))
    spreads = {}
    factors = {'L0_conv_w_real': 8.0, 'L0_conv_w_imag': 8.0, 'L1_conv_weight': 4.816}
    for name, (base, spread) in spreads.items():
        noise = np.random.default_rng([zlib.crc32(name.encode()), seed]).standard_normal(out[name].shape)
        drawn = base * np.exp(spread * noise) if base else spread * noise
        out[name] = jnp.asarray(drawn.astype(out[name].dtype))
    for name, factor in factors.items():
        out[name] = (out[name] * factor).astype(out[name].dtype)
    return out
```

```python
import concourse.bass as bass
from concourse import mybir
from contextlib import ExitStack

B, C, H, W = 16, 32, 256, 256
N = H * W
M = 16
P = 128
EPS = 1e-5
K3 = 3
FFT = 512
CUT = (FFT - H) // 2
OUTW = H + K3 - 1 - CUT
NBLK = 33
COL0 = W - 4 * NBLK
TAPW = 4 + K3 - 1
X_UP = 4096.0
W_UP = 1024.0
O_DOWN = 2.0 ** -13
T_DOWN = 2.0 ** -4
E_UP = 1024.0
G_UP = 64.0
K_UP = 1024.0


def bass_spectral_then_conv(nc: bass.Bass, x, w_real, w_imag, conv_w, conv_b,
                            cf_d, l_d, cst_d, e_d, ident_d, rep_d, msc_d, mcd_d, mg_d, dw_d, sel_d, out, samples=B):
    f32, f16 = mybir.dt.float32, mybir.dt.float16
    ALU, ACT, AX = mybir.AluOpType, mybir.ActivationFunctionType, mybir.AxisListType
    ctx = ExitStack()
    with ctx:
        def sb(name, shape, dt):
            return ctx.enter_context(nc.sbuf_tensor(name, shape, dt))

        def sem(name):
            return ctx.enter_context(nc.semaphore(name))

        img = [sb(f"img{k}", [P, 2, C, W], f32) for k in range(2)]
        wmix = sb("wmix", [P, 2, 2, M, P], f16)
        colsum = sb("colsum", [P, 2, 512], f32)
        shared = sb("shared", [P, 2048], f32)
        turned = shared[:, :].rearrange("p (h m c) -> p h m c", h=2, m=32)
        obroad = shared[:, 0:1024].rearrange("p (k c f) -> p k c f", k=8, c=4)
        ospec = shared[0:32, 0:512]
        prod_ox = shared[0:32, 512:1024]
        prod_oo = shared[0:32, 1024:1536]
        junk = shared[:, 1536:2048]
        trow = [shared[:, 256 * k:256 * k + 256].bitcast(f16) for k in range(2)]
        znorm = [shared[:, 512 + 512 * k:1024 + 512 * k] for k in range(2)]
        stats = sb("stats", [P, C, 6], f32)
        moments = sb("moments", [P, 2, C, 2], f32)
        meansq = sb("meansq", [P, C, 2], f32)
        xnorm = sb("xnorm", [P, 4, M, 2], f32)
        xtri = sb("xtri", [P, M, 2, 4, 3], f16)
        xdiag = sb("xdiag", [P, M * 2, 4, 12], f16)
        opair = sb("opair", [P, 2, 4, M, 2], f32)
        ostat = sb("ostat", [P, C, 32], f16)
        edge = sb("edge", [P, 2, 9 * P], f32)
        edgeT = sb("edgeT", [2 * NBLK, P], f32)
        gn = sb("gn", [P, 2, NBLK, OUTW], f16)
        edge_out = sb("edge_out", [NBLK, 2, P], f32)
        wconv = sb("wconv", [P, 2, K3, TAPW * C], f16)
        bias_rows = sb("bias_rows", [P, C], f32)
        bias_half = sb("bias_half", [P, C], f16)
        cf = sb("cf", [P, 2, 32], f32)
        lt = sb("lt", [P, 4, 96], f32)
        cst = sb("cst", [P, W], f16)
        et = sb("et", [P, 2, P], f16)
        ident = sb("ident", [P, P], f32)
        ones = sb("ones", [P, P], f32)
        rep = sb("rep", [C, P], f32)
        mask_sc = sb("mask_sc", [P, C, 2], f32)
        mask_cd = sb("mask_cd", [P, C, 2], f32)
        mask_g = sb("mask_g", [P, C], f32)
        dw_is = sb("dw_is", [P, 4], f32)
        sel = sb("sel", [32, 2 * P], f32)
        nu = sb("nu", [P, 12], f32)
        sc = sb("sc", [P, 32], f32)
        bank = [ctx.enter_context(nc.psum_tensor(f"bank{k}", [P, 512], f32)) for k in range(8)]

        MAXES, NU0, RNU0, NU1, RNU1, ALPHA, BETA, NUV, NUV2, NUM, BIAS_CD = range(11)
        MU, MS, MUSQ, VAR, VE, RS = 0, 2, 4, 6, 8, 10
        XS, DC, DOX, DOO, U0, SIG, A0, A1, A2, GS, GB = range(12, 23)
        ROOT, ROOT2 = 24, 26

        def col(t, k, n=1):
            return t[:, k:k + n]

        tables_in = sem("tables_in")
        weights_in = sem("weights_in")
        bias_in = sem("bias_in")
        ones_set = sem("ones_set")
        peak_col = sem("peak_col")
        peak_row = sem("peak_row")
        peak_got = sem("peak_got")
        peak_all = sem("peak_all")
        nu_set = sem("nu_set")
        conv_rep = sem("conv_rep")
        mix_hi = sem("mix_hi")
        weights_done = sem("weights_done")
        cleared = sem("cleared")
        loaded = [[sem(f"loaded{k}{q}") for q in range(4)] for k in range(2)]
        cols_mm = sem("cols_mm")
        cols_sb = sem("cols_sb")
        turn_mm = sem("turn_mm")
        turn_sb = sem("turn_sb")
        moments_ready = sem("moments_ready")
        sums_mm = sem("sums_mm")
        var_ready = sem("var_ready")
        dev_ready = sem("dev_ready")
        var1_ready = sem("var1_ready")
        dev1_ready = sem("dev1_ready")
        spec_mm = sem("spec_mm")
        spec_read = sem("spec_read")
        xtri_ready = sem("xtri_ready")
        xdiag_ready = sem("xdiag_ready")
        mix_mm = sem("mix_mm")
        obroad_ready = sem("obroad_ready")
        oturn_mm = sem("oturn_mm")
        xturn_mm = sem("xturn_mm")
        ostat_hi = sem("ostat_hi")
        ostat_ready = sem("ostat_ready")
        prods_ready = sem("prods_ready")
        s2_mm = sem("s2_mm")
        s2_read = sem("s2_read")
        znorm_scalars = sem("znorm_scalars")
        t_mm = sem("t_mm")
        t_hi = sem("t_hi")
        t_lo = sem("t_lo")
        s_mm = sem("s_mm")
        x1_added = sem("x1_added")
        edge_packed = sem("edge_packed")
        edge_moved = sem("edge_moved")
        corner_mm = sem("corner_mm")
        z_ready = sem("z_ready")
        g_hi = sem("g_hi")
        g_lo = sem("g_lo")
        edge_mm = sem("edge_mm")
        edge_sb = sem("edge_sb")
        edge_back = [sem(f"edge_back{k}") for k in range(2)]
        edge_added = sem("edge_added")
        conv_mm = sem("conv_mm")
        conv_added = sem("conv_added")
        stored = [[sem(f"stored{t}{q}") for q in range(4)] for t in range(2)]
        act_step = sem("act_step")
        dve_step = sem("dve_step")
        dve_setup = sem("dve_setup")
        pe_setup = sem("pe_setup")

        EDGE_J = [(0, 8), (8, 16), (16, 24), (24, NBLK)]
        CORNER = [(4 * k, min(4 * k + 4, NBLK)) for k in range(9)]

        xr = x.rearrange("b (q c) (t p) w -> b t q p c w", q=4, t=2)
        outr = out.rearrange("b (q c) (t p) w -> b t q p c w", q=4, t=2)
        LAST = samples - 1
        PAIRS = (samples - 2) // 2

        def over_samples(eng, step):
            step(0, 0, 0)
            if PAIRS:
                with eng.Fori(0, PAIRS) as p:
                    step(2 * p + 1, p, 1)
                    step(2 * p + 2, p + 1, 0)
            step(LAST, LAST // 2, 1)

        def corner(v, half):
            if v < 9:
                j0, j1 = CORNER[v]
                w = P * (j1 - j0)
                return znorm[v % 2][:, 0:w], w, gn[:, half, j0:j1, 2:OUTW]
            return znorm[v % 2][:, 0:2 * NBLK], 2 * NBLK, gn[:, half, :, 0:2]

        def corner_in(z, v):
            return z.rearrange("p (j h) -> p j h", h=P) if v < 9 else z.rearrange("p (r j) -> p j r", r=2)

        block = ctx.enter_context(nc.Block())

        @block.sync
        def _(sp):
            for dst, src in ((cf, cf_d), (lt, l_d), (cst, cst_d), (et, e_d), (ident, ident_d), (rep, rep_d),
                             (mask_sc, msc_d), (mask_cd, mcd_d), (mask_g, mg_d), (dw_is, dw_d), (sel, sel_d)):
                sp.dma_start(dst[:], src).then_inc(tables_in, 16)
            sp.dma_start(shared[0:C, 0:288].rearrange("c (o k) -> c o k", k=9),
                         conv_w.rearrange("o c a b -> c o (a b)")).then_inc(weights_in, 16)
            sp.dma_start(nu[0:C, BIAS_CD:BIAS_CD + 1], conv_b.rearrange("(c a) -> c a", a=1)).then_inc(weights_in, 16)
            for s in range(4):
                for ri, w in enumerate((w_real, w_imag)):
                    sp.dma_start(img[1][32 * s:32 * s + 32, ri].rearrange("p c w -> p (c w)"),
                                 w.rearrange("i o m n -> i (o m n)")).then_inc(weights_in, 16)
            for q in range(4):
                for t in range(2):
                    sp.dma_start(img[0][:, t, 8 * q:8 * q + 8, :], xr[0, t, q]).then_inc(loaded[0][q], 16)
            sp.wait_ge(weights_done, 2)
            for q in range(4):
                for t in range(2):
                    sp.dma_start(img[1][:, t, 8 * q:8 * q + 8, :], xr[1, t, q]).then_inc(loaded[1][q], 16)

            def turn_over(n, k, load):
                def out_and_in(t):
                    for q in (3, 2, 1, 0):
                        sp.dma_start(outr[n - 1, t, q], img[1 - k][:, t, 8 * q:8 * q + 8, :]).then_inc(stored[t][q], 16)
                    for group in ((3,), (2,), (1, 0)) if load else ():
                        for q in group:
                            sp.wait_ge(stored[t][q], 16 * n)
                        for q in group:
                            sp.dma_start(img[1 - k][:, t, 8 * q:8 * q + 8, :], xr[n + 1, t, q]).then_inc(loaded[1 - k][q], 16)

                sp.wait_ge(edge_added, 4 * n)
                out_and_in(1)
                sp.wait_ge(conv_added, 9 * n)
                out_and_in(0)

            if PAIRS:
                with sp.Fori(2, PAIRS + 2) as p:
                    turn_over(2 * p - 3, 1, True)
                    turn_over(2 * p - 2, 0, True)
            turn_over(LAST, 1, False)
            turn_over(samples, 0, False)
            for t in range(2):
                for q in range(4):
                    sp.wait_ge(stored[t][q], 16 * samples)

        @block.tensor
        def _(pe):
            def setup():
                pe.wait_ge(tables_in, 176)
                pe.wait_ge(peak_col, 2)
                nc.tensor.matmul(bank[0][0:1, 0:P], col(sc, 0), ident[:, :], start=True, stop=True)
                nc.tensor.matmul(bank[0][0:1, P:2 * P], col(sc, 1), ident[:, :], start=True, stop=True).then_inc(peak_row, 1)
                pe.wait_ge(ones_set, 1)
                pe.wait_ge(peak_got, 1)
                nc.tensor.matmul(bank[1][:, 0:2], ones[0:1, :], sc[0:1, 2:4], start=True, stop=True).then_inc(peak_all, 1)
                nc.tensor.matmul(bank[2][:, 0:288], rep[:, :], shared[0:C, 0:288], start=True, stop=True)
                nc.tensor.matmul(bank[3][:, 0:1], rep[:, :], nu[0:C, BIAS_CD:BIAS_CD + 1], start=True, stop=True)\
                    .then_inc(conv_rep, 1)

            def conv_edge(n):
                pe.wait_ge(g_lo, 10 * n + 10)
                for i in range(2):
                    pairs = [(OUTW - 1, 1), (OUTW - 2, 2)] if i == 0 else [(OUTW - 1, 2)]
                    terms = [(r, a, gh, wh) for r, a in pairs for gh, wh in ((0, 0), (0, 1), (1, 0))]
                    for k, (r, a, gh, wh) in enumerate(terms):
                        nc.tensor.matmul(bank[6][0:NBLK, i * P:i * P + 64], gn[:, gh, :, r],
                                         wconv[:, wh, a, 4 * C:6 * C], start=(k == 0), stop=False, skip_group_check=True)
                        last = nc.tensor.matmul(bank[6][0:NBLK - 1, i * P:i * P + P], gn[:, gh, 1:NBLK, r],
                                                wconv[:, wh, a, 0:4 * C], start=False, stop=(k == len(terms) - 1),
                                                skip_group_check=True)
                last.then_inc(edge_mm, 1)

            def conv_bank(n, u):
                if u == 0:
                    pe.wait_ge(g_lo, 10 * n + 10)
                if u >= 2:
                    pe.wait_ge(conv_added, 9 * n + u - 1)
                ps = bank[4 + u % 2]
                jobs = []
                for j in range(4 * u, min(4 * u + 5, NBLK)):
                    lo = 0 if j > 4 * u else 4
                    hi = TAPW if j < 4 * u + 4 else 4
                    at = (j - 1 - 4 * u + (1 if lo else 0)) * P
                    for gh, wh in ((0, 0), (0, 1), (1, 0)):
                        jobs += [(j, a, gh, wh, lo, hi, at) for a in range(K3)]
                for k, (j, a, gh, wh, lo, hi, at) in enumerate(jobs):
                    last = nc.tensor.matmul(ps[:, at:at + (hi - lo) * C], gn[:, gh, j, 2 - a:2 - a + P],
                                            wconv[:, wh, a, lo * C:hi * C], start=(k == 0), stop=(k == len(jobs) - 1),
                                            skip_group_check=True)
                last.then_inc(conv_mm, 1)

            def step(n, use, k):
                prev = n - 1
                has_prev = not isinstance(n, int) or n > 0
                for q in range(4):
                    pe.wait_ge(loaded[k][q], 32 * (use + 1))
                    if q > 0 or has_prev:
                        pe.wait_ge(cols_sb, 4 * n + q)
                    if q == 0 and has_prev:
                        pe.wait_ge(z_ready, 10 * n)
                    for t in range(2):
                        for j in range(4):
                            last = nc.tensor.matmul(
                                bank[0][32 * j:32 * j + 32, :], cf[:, t, :],
                                img[k][:, t, 8 * q + j:8 * q + j + 5:4, :], start=(t == 0), stop=(t == 1))
                    last.then_inc(cols_mm, 1)
                    if has_prev:
                        if q == 0:
                            conv_edge(prev)
                        conv_bank(prev, q)
                    pe.wait_ge(cols_sb, 4 * n + q + 1)
                    if q > 0 or has_prev:
                        pe.wait_ge(turn_sb, 4 * n + q)
                    for e in range(2):
                        for h in range(2):
                            last = nc.tensor.transpose(bank[1][:, (h * 2 + e) * P:(h * 2 + e + 1) * P],
                                                       colsum[:, q % 2, e * W + h * P:e * W + h * P + P], ident[:, :])
                    last.then_inc(turn_mm, 1)
                pe.wait_ge(moments_ready, n + 1)
                nc.tensor.matmul(bank[2][:, 0:P], ones[:, :], moments[:, :, :, :], start=True, stop=True).then_inc(sums_mm, 1)
                pe.wait_ge(turn_sb, 4 * n + 4)
                for g in range(4):
                    for k4 in range(4):
                        ab, h = k4 // 2, k4 % 2
                        last = nc.tensor.matmul(bank[3][:, 32 * g:32 * g + 96],
                                                turned[:, h, 16 * ab + 4 * g:16 * ab + 4 * g + 4, :],
                                                lt[:, k4, :], start=(k4 == 0), stop=(k4 == 3))
                last.then_inc(spec_mm, 1)
                if has_prev:
                    conv_bank(prev, 4)
                    conv_bank(prev, 5)
                pe.wait_ge(xdiag_ready, 4 * n + 4)
                pe.wait_ge(spec_read, n + 1)
                for m in range(M):
                    terms = [(ri, wh, xh) for wh, xh in ((0, 0), (0, 1), (1, 0)) for ri in range(2)]
                    for t, (ri, wh, xh) in enumerate(terms):
                        rhs = xdiag[:, 2 * m + xh].rearrange("p s (g e) -> p (s g) e", e=3)[:, :, ri:ri + 2]
                        last = nc.tensor.matmul(bank[3][:, 32 * m:32 * m + 32], wmix[:, wh, ri, m, :], rhs,
                                                start=(t == 0), stop=(t == len(terms) - 1))
                last.then_inc(mix_mm, 1)
                if has_prev:
                    conv_bank(prev, 6)
                pe.wait_ge(obroad_ready, n + 1)
                for ri in range(2):
                    for s in range(4):
                        last = nc.tensor.transpose(bank[ri][:, P * s:P * s + P],
                                                   obroad[:, 4 * ri + s].rearrange("p c f -> p (c f)"), ident[:, :])
                last.then_inc(oturn_mm, 1)
                for g in range(4):
                    last = nc.tensor.transpose(bank[3][0:32, P * g:P * g + P], xnorm[:, g], ident[:, :])
                last.then_inc(xturn_mm, 1)
                if has_prev:
                    conv_bank(prev, 7)
                    conv_bank(prev, 8)
                pe.wait_ge(prods_ready, n + 1)
                if has_prev:
                    pe.wait_ge(edge_sb, n)
                nc.tensor.matmul(bank[2][:, 128:128 + C], sel[:, 0:P], ospec[:, 0:C], start=True, stop=True)
                nc.tensor.matmul(bank[6][:, :], ones[0:32, :], prod_ox, start=True, stop=True)
                nc.tensor.matmul(bank[7][:, :], ones[0:32, :], prod_oo, start=True, stop=True).then_inc(s2_mm, 1)
                pe.wait_ge(ostat_ready, n + 1)

                def over_w(r):
                    if r >= 2:
                        pe.wait_ge(t_lo, 16 * n + r - 1)
                    for o in range(2):
                        for c in range(4):
                            last = nc.tensor.matmul(bank[r % 2][32 * c:32 * c + 32, o * W:o * W + W],
                                                    ostat[:, 2 * r + o, :], cst[:, :], start=True, stop=True)
                    last.then_inc(t_mm, 1)

                def over_h(r):
                    pe.wait_ge(t_lo, 16 * n + r + 1)
                    for t in range(2):
                        v = 2 * r + t
                        if v >= 4:
                            pe.wait_ge(x1_added, 32 * n + v - 3)
                        elif v == 0:
                            pe.wait_ge(s2_read, n + 1)
                            if has_prev:
                                pe.wait_ge(conv_added, 9 * n)
                        nc.tensor.matmul(bank[4 + v % 4][:, :], et[:, t, :], trow[r % 2], start=True, stop=True)\
                            .then_inc(s_mm, 1)

                over_w(0)
                for r in range(1, 16):
                    over_w(r)
                    over_h(r - 1)
                over_h(15)
                pe.wait_ge(x1_added, 32 * n + 32)
                for v, (j0, j1) in enumerate(CORNER):
                    if v >= 2:
                        pe.wait_ge(z_ready, 10 * n + v - 1)
                    for j in range(j0, j1):
                        for d in range(4):
                            last = nc.tensor.matmul(bank[v % 2][32 * d:32 * d + 32, P * (j - j0):P * (j - j0) + P],
                                                    img[k][:, 1, :, COL0 + 4 * j + d], ident[:, :], start=True, stop=True)
                    last.then_inc(corner_mm, 1)
                pe.wait_ge(edge_moved, 64 * n + 64)
                pe.wait_ge(z_ready, 10 * n + 8)
                nc.tensor.transpose(bank[1][:, 0:2 * NBLK], edgeT[:, :], ident[0:2 * NBLK, 0:2 * NBLK])\
                    .then_inc(corner_mm, 1)

            setup()
            over_samples(pe, step)
            conv_edge(LAST)
            for u in range(9):
                conv_bank(LAST, u)

        @block.scalar
        def _(act):
            def edge_out_copy(n):
                act.wait_ge(edge_mm, n + 1)
                src = bank[6][:, 0:2 * P].rearrange("p (i f) -> p i f", i=2)
                nc.scalar.activation(edge_out[0:32, :, :], src[0:32], ACT.Copy, scale=nu[0:32, BETA:BETA + 1])
                nc.scalar.activation(edge_out[32:33, :, 0:64], src[32:33, :, 0:64], ACT.Copy,
                                     scale=nu[32:33, BETA:BETA + 1]).then_inc(edge_sb, 1)
                act.wait_ge(edge_sb, n + 1)

            def edge_out_send(n, first):
                for q in (first, first + 1):
                    j0, j1 = EDGE_J[q]
                    if q >= 2:
                        act.wait_ge(edge_added, 4 * n + q - 1)
                    for i in range(2):
                        act.dma_start(edge[i:i + 1, q % 2, 0:P * (j1 - j0)].rearrange("p (j f) -> p j f", f=P),
                                      edge_out[j0:j1, i, :]).then_inc(edge_back[q % 2], 16)

            act.wait_ge(nu_set, 1)
            for ri in range(2):
                for s in range(4):
                    rows = slice(32 * s, 32 * s + 32)
                    src = img[1][rows, ri].rearrange("p c w -> p (c w)").rearrange("p (o g s n) -> p s n g o", o=C, g=4, s=4)[:, s]
                    dst = wmix[rows, 0, ri].rearrange("p n (g o) -> p n g o", g=4)
                    nc.scalar.activation(dst, src, ACT.Copy, scale=nu[rows, RNU0:RNU0 + 1]).then_inc(mix_hi, 1)

            def step(n, use, k):
                has_prev = not isinstance(n, int) or n > 0
                for q in range(4):
                    act.wait_ge(cols_mm, 4 * n + q + 1)
                    if q >= 2:
                        act.wait_ge(turn_mm, 4 * n + q - 1)
                    elif has_prev:
                        act.wait_ge(turn_mm, 4 * n)
                    nc.scalar.activation(colsum[:, q % 2, :], bank[0][:, :], ACT.Copy).then_inc(cols_sb, 1)
                    if q == 0 and has_prev:
                        edge_out_copy(n - 1)
                    if q in (0, 2) and has_prev:
                        edge_out_send(n - 1, q)
                    act.wait_ge(turn_mm, 4 * n + q + 1)
                    if q == 0 and has_prev:
                        act.wait_ge(g_lo, 10 * n)
                    elif q == 0:
                        act.wait_ge(weights_done, 2)
                    dst = turned[:, :, :, 8 * q:8 * q + 8].rearrange("p h m c -> p h c m")
                    nc.scalar.activation(dst, bank[1][:, :].rearrange("p (h c m) -> p h c m", h=2, c=8),
                                         ACT.Copy).then_inc(turn_sb, 1)
                act.wait_ge(var_ready, n + 1)
                nc.scalar.activation(col(sc, ROOT, 2), col(sc, VE, 2), ACT.Sqrt).then_inc(dev_ready, 1)
                act.wait_ge(xtri_ready, n + 1)
                if has_prev:
                    act.wait_ge(mix_mm, n)
                for s in range(4):
                    rows = slice(32 * s, 32 * s + 32)
                    nc.scalar.activation(xdiag[rows, :, s, :], xtri[rows].rearrange("p n h g e -> p (n h) (g e)"),
                                         ACT.Copy).then_inc(xdiag_ready, 1)
                act.wait_ge(mix_mm, n + 1)
                for g in range(4):
                    rows = slice(32 * g, 32 * g + 32)
                    src = bank[3][rows, :].rearrange("p (n s g e) -> p g s n e", n=M, s=4, g=4)[:, g]
                    nc.scalar.activation(opair[rows, 1], src, ACT.Copy).then_inc(act_step, 1)
                act.wait_ge(act_step, 6 * n + 4)
                pairs = opair[:, :, :, :, :].rearrange("p r s n e -> p r (s n) e")
                nc.scalar.activation(pairs[:, 0, :, 0], pairs[:, 1, :, 1], ACT.Copy).then_inc(act_step, 1)
                nc.scalar.activation(pairs[:, 0, :, 1], pairs[:, 1, :, 0], ACT.Copy, scale=-1.0).then_inc(act_step, 1)
                act.wait_ge(act_step, 6 * n + 6)
                src = opair[:, :, :, :, :].rearrange("p r s n e -> p (r s) (n e)").unsqueeze(2).broadcast_to([P, 8, 4, 32])
                nc.scalar.activation(obroad, src, ACT.Copy).then_inc(obroad_ready, 1)
                act.wait_ge(oturn_mm, n + 1)
                for ri in range(2):
                    dst = ostat[:, :, :].rearrange("p o (g r s) -> p r s g o", g=4, r=2)[:, ri]
                    nc.scalar.activation(dst, bank[ri][:, :].rearrange("p (s g o) -> p s g o", s=4, g=4),
                                         ACT.Copy, scale=O_DOWN).then_inc(ostat_hi, 1)
                for r in range(17):
                    if r < 16:
                        act.wait_ge(t_mm, 16 * n + r + 1)
                        if r == 0:
                            act.wait_ge(s2_mm, n + 1)
                        if r >= 2:
                            act.wait_ge(s_mm, 32 * n + 2 * (r - 1))
                        nc.scalar.activation(trow[r % 2], bank[r % 2][:, :], ACT.Copy, scale=T_DOWN).then_inc(t_hi, 1)
                    if r == 5:
                        act.wait_ge(var1_ready, n + 1)
                        nc.scalar.activation(col(sc, ROOT), col(sc, A0), ACT.Sqrt).then_inc(dev1_ready, 1)
                    if r in (8, 16):
                        q = r // 8 - 1
                        act.wait_ge(x1_added, 32 * n + 16 * q + 16)
                        if q > 0:
                            act.wait_ge(edge_moved, 64 * n + 32)
                        elif has_prev:
                            act.wait_ge(edge_moved, 64 * n)
                        dst = edge[96:P, :, :].rearrange("p a b -> p (a b)")[:, 0:NBLK * 64]\
                            .rearrange("p (j c) -> p j c", c=16)
                        src = img[k][96:P, 0, 16 * q:16 * q + 16, COL0:W].rearrange("p c w -> p w c")
                        nc.scalar.activation(dst, src, ACT.Copy).then_inc(edge_packed, 1)
                        act.wait_ge(edge_packed, 2 * n + q + 1)
                        if q == 0 and has_prev:
                            act.wait_ge(corner_mm, 10 * n)
                        for i in range(2):
                            act.dma_start(
                                edgeT[NBLK * i:NBLK * i + NBLK, :].rearrange("p (d c) -> p d c", d=4)[:, :, 16 * q:16 * q + 16],
                                edge[P - 2 + i:P - 1 + i, :, :].rearrange("p a b -> p (a b)")[:, 0:NBLK * 64]
                                .rearrange("p (j d c) -> p j d c", d=4, c=16)).then_inc(edge_moved, 16)
                if has_prev:
                    act.wait_ge(edge_added, 4 * n)
                act.wait_ge(znorm_scalars, n + 1)
                if has_prev:
                    act.wait_ge(conv_mm, 9 * n)
                for v in range(10):
                    act.wait_ge(corner_mm, 10 * n + v + 1)
                    if v >= 2:
                        act.wait_ge(g_lo, 10 * n + v - 1)
                    z, w, dst = corner(v, 0)
                    src = bank[v % 2][:, 0:w]
                    nc.scalar.activation(z, src, ACT.Identity, bias=col(sc, GB), scale=col(sc, GS)).then_inc(z_ready, 1)
                    act.wait_ge(z_ready, 10 * n + v + 1)
                    nc.scalar.activation(dst, corner_in(z, v), ACT.Copy).then_inc(g_hi, 1)

            over_samples(act, step)
            edge_out_copy(LAST)
            edge_out_send(LAST, 0)
            edge_out_send(LAST, 2)

        @block.gpsimd
        def _(pool):
            nc.gpsimd.memset(xdiag[:, :, :, :], 0.0).then_inc(cleared, 1)
            nc.gpsimd.memset(edge_out[:, :, :], 0.0).then_inc(cleared, 1)
            nc.gpsimd.memset(bias_rows[:, :], 0.0).then_inc(cleared, 1)
            pool.wait_ge(cleared, 3)
            for c in range(4):
                pool.dma_start(bias_rows[32 * c:32 * c + 1, :], conv_b.rearrange("(a c) -> a c", a=1)).then_inc(bias_in, 16)

            def edge_add(n, k):
                for q, (j0, j1) in enumerate(EDGE_J):
                    w0, w1 = 4 * j0, min(4 * j1, OUTW)
                    pool.wait_ge(edge_back[q % 2], 64 * n + 32 * (q // 2) + 32)
                    rows = img[k][0:2, 1, :, w0:w1]
                    src = edge[0:2, q % 2, 0:C * (w1 - w0)].rearrange("p (w o) -> p o w", o=C)
                    nc.gpsimd.tensor_tensor(rows, rows, src, ALU.add).then_inc(edge_added, 1)

            def step(n, use, k):
                if not isinstance(n, int) or n > 0:
                    edge_add(n - 1, 1 - k)

            over_samples(pool, step)
            edge_add(LAST, 1)

        @block.vector
        def _(dve):
            nc.vector.memset(ones[:, :], 1.0).then_inc(ones_set, 1)
            count = [0]

            def link(ins):
                count[0] += 1
                ins.then_inc(dve_setup, 1)
                dve.wait_ge(dve_setup, count[0])

            def setup():
                dve.wait_ge(weights_in, 160)
                nc.vector.tensor_reduce(col(sc, 4), img[1][:, :, :, :].rearrange("p t c w -> p (t c w)"), AX.X, ALU.max)\
                    .then_inc(dve_setup, 1)
                nc.vector.tensor_reduce(col(sc, 5), img[1][:, :, :, :].rearrange("p t c w -> p (t c w)"), AX.X, ALU.min)\
                    .then_inc(dve_setup, 1)
                nc.vector.memset(col(sc, 6, 4), 0.0).then_inc(dve_setup, 1)
                count[0] += 3
                dve.wait_ge(dve_setup, 3)
                link(nc.vector.tensor_reduce(sc[0:C, 6:7], shared[0:C, 0:288], AX.X, ALU.max))
                link(nc.vector.tensor_reduce(sc[0:C, 7:8], shared[0:C, 0:288], AX.X, ALU.min))
                link(nc.vector.tensor_reduce(sc[0:C, 8:9], nu[0:C, BIAS_CD:BIAS_CD + 1], AX.X, ALU.max))
                nc.vector.scalar_tensor_tensor(col(sc, 1), col(sc, 7), -1.0, col(sc, 6), ALU.mult, ALU.max).then_inc(peak_col, 1)
                link(nc.vector.scalar_tensor_tensor(col(sc, 5), col(sc, 5), -1.0, col(sc, 4), ALU.mult, ALU.max))
                link(nc.vector.scalar_tensor_tensor(col(sc, 9), col(sc, 8), -1.0, col(sc, 8), ALU.mult, ALU.max))
                nc.vector.scalar_tensor_tensor(col(sc, 0), col(sc, 9), 1.0 / 64, col(sc, 5), ALU.mult, ALU.max).then_inc(peak_col, 1)
                dve.wait_ge(peak_row, 1)
                nc.vector.tensor_reduce(sc[0:1, 2:4], bank[0][0:1, 0:2 * P].rearrange("p (k f) -> p k f", k=2), AX.X, ALU.max)\
                    .then_inc(peak_got, 1)
                dve.wait_ge(peak_all, 1)
                link(nc.vector.tensor_scalar(nu[:, NU0:NU0 + 3:2], bank[1][:, 0:2], 1e-30, None, ALU.max))
                link(nc.vector.reciprocal(col(sc, 6), col(nu, NU0)))
                link(nc.vector.reciprocal(col(sc, 7), col(nu, NU1)))
                link(nc.vector.tensor_scalar(col(nu, RNU0), col(sc, 6), W_UP, None, ALU.mult))
                link(nc.vector.tensor_scalar(col(nu, RNU1), col(sc, 7), K_UP, None, ALU.mult))
                nc.vector.tensor_scalar(col(nu, ALPHA), col(nu, NU0), O_SCALE_INV, None, ALU.mult)
                link(nc.vector.tensor_scalar(col(nu, BETA), col(nu, NU1), 1.0 / (FFT * G_UP * K_UP), None, ALU.mult))
                nc.vector.tensor_scalar(col(nu, NUV), col(nu, NU0), 2.0 ** -34, None, ALU.mult)
                link(nc.vector.tensor_scalar(col(nu, NUM), col(nu, NU0), 2.0 ** -23, None, ALU.mult))
                link(nc.vector.tensor_tensor(col(nu, NUV2), col(nu, NUM), col(nu, NUM), ALU.mult))
                dve.wait_ge(conv_rep, 1)
                dve.wait_ge(tables_in, 176)
                nc.vector.tensor_copy(col(nu, BIAS_CD), bank[3][:, 0:1]).then_inc(nu_set, 1)
                taps = shared[:, 0:288].rearrange("p (a b o) -> p a b o", a=3, b=3)
                wide = shared[:, 512:512 + K3 * TAPW * C].rearrange("p (a f) -> p a f", a=3)
                link(nc.vector.tensor_scalar(taps, bank[2][:, 0:288].rearrange("p (o a b) -> p a b o", a=3, b=3),
                                             col(nu, RNU1), None, ALU.mult))
                link(nc.vector.memset(wide, 0.0))
                for d in range(4):
                    for a in range(K3):
                        part = wide[:, a, d * C:(d + 3) * C]
                        link(nc.vector.scalar_tensor_tensor(part, taps[:, a].rearrange("p b o -> p (b o)"),
                                                            col(dw_is, d), part, ALU.mult, ALU.add))
                link(nc.vector.tensor_copy(wconv[:, 0], wide))
                link(nc.vector.tensor_tensor(wconv[:, 1], wide, wconv[:, 0], ALU.subtract))
                dve.wait_ge(bias_in, 64)
                link(nc.vector.tensor_scalar(bias_rows[:, :], bias_rows[:, :], col(nu, RNU0), 2.0 ** 9 / W_UP, ALU.mult, ALU.mult))
                link(nc.vector.tensor_copy(bias_half[:, :], bias_rows[:, :]))
                link(nc.vector.tensor_tensor(bias_half[64:P, :], bias_rows[64:P, :], bias_half[64:P, :], ALU.subtract))
                for ri in range(2):
                    for s in range(4):
                        dve.wait_ge(mix_hi, 4 * ri + s + 1)
                        rows = slice(32 * s, 32 * s + 32)
                        for g in range(4):
                            src = img[1][rows, ri].rearrange("p c w -> p (c w)")\
                                .rearrange("p (o g s n) -> p g s n o", o=C, g=4, s=4)[:, g, s]
                            hi, lo = (wmix[rows, h, ri].rearrange("p n (g o) -> p g n o", g=4)[:, g] for h in range(2))
                            last = nc.vector.scalar_tensor_tensor(lo, src, nu[rows, RNU0:RNU0 + 1], hi, ALU.mult, ALU.subtract)
                    last.then_inc(weights_done, 1)
                dve.wait_ge(cleared, 3)

            def conv_add(n, k, u):
                dve.wait_ge(conv_mm, 9 * n + u + 1)
                if u == 0:
                    dve.wait_ge(edge_packed, 2 * n + 2)
                w = min(16, OUTW - 16 * u)
                x1 = img[k][:, 0, :, 16 * u:16 * u + w]
                ps = bank[4 + u % 2][:, 0:w * C].rearrange("p (w o) -> p o w", o=C)
                nc.vector.scalar_tensor_tensor(x1, ps, col(nu, BETA), x1, ALU.mult, ALU.add).then_inc(conv_added, 1)

            def step(n, use, k):
                has_prev = not isinstance(n, int) or n > 0
                at = [0]

                def then(ins):
                    at[0] += 1
                    ins.then_inc(dve_step, 1)
                    dve.wait_ge(dve_step, STEPS * n + at[0])

                def rsqrt(to, v, m, asked, root):
                    dve.wait_ge(asked, n + 1)
                    dve.wait_ge(root, n + 1)
                    then(nc.vector.reciprocal(col(sc, to, m), col(sc, ROOT, m)))
                    then(nc.vector.tensor_tensor(col(sc, ROOT2, m), col(sc, to, m), col(sc, to, m), ALU.mult))
                    then(nc.vector.tensor_tensor(col(sc, ROOT2, m), col(sc, ROOT2, m), col(sc, v, m), ALU.mult))
                    then(nc.vector.tensor_scalar(col(sc, ROOT2, m), col(sc, ROOT2, m), -0.5, 1.5, ALU.mult, ALU.add))
                    then(nc.vector.tensor_tensor(col(sc, to, m), col(sc, to, m), col(sc, ROOT2, m), ALU.mult))

                for q in range(4):
                    dve.wait_ge(loaded[k][q], 32 * (use + 1))
                    for c in range(8 * q, 8 * q + 8):
                        last = nc.vector.bn_stats(stats[:, c, :], img[k][:, :, c, :])
                    if q == 3:
                        then(last)
                    if has_prev:
                        conv_add(n - 1, 1 - k, q)
                mean, var = stats[:, :, 1:5:3], stats[:, :, 2:6:3]
                then(nc.vector.tensor_tensor(meansq[:, :, :], mean, mean, ALU.mult))
                if has_prev:
                    dve.wait_ge(sums_mm, n)
                nc.vector.tensor_copy(moments[:, 0], mean)
                nc.vector.scalar_tensor_tensor(moments[:, 1], var, 1.0 / 256, meansq[:, :, :], ALU.mult, ALU.add)\
                    .then_inc(moments_ready, 1)
                dve.wait_ge(moments_ready, n + 1)
                dve.wait_ge(sums_mm, n + 1)
                for kind, to in ((0, MU), (1, MS)):
                    for lay, mask in ((0, mask_sc), (1, mask_cd)):
                        then(nc.vector.tensor_tensor_reduce(
                            out=meansq[:, :, :].rearrange("p c e -> p (c e)"), in0=bank[2][:, 64 * kind:64 * kind + 64],
                            in1=mask[:, :, :].rearrange("p c e -> p (c e)"), scale=1.0, scalar=0.0,
                            op0=ALU.mult, op1=ALU.add, accum_out=col(sc, to + lay)))
                then(nc.vector.tensor_tensor(col(sc, MUSQ, 2), col(sc, MU, 2), col(sc, MU, 2), ALU.mult))
                then(nc.vector.tensor_tensor(col(sc, VAR, 2), col(sc, MS, 2), col(sc, MUSQ, 2), ALU.subtract))
                nc.vector.tensor_scalar(col(sc, VE, 2), col(sc, VAR, 2), 0.0, EPS, ALU.max, ALU.add).then_inc(var_ready, 1)
                rsqrt(RS, VE, 2, var_ready, dev_ready)
                nc.vector.tensor_scalar(col(sc, XS), col(sc, RS), X_UP / N, None, ALU.mult)
                then(nc.vector.scalar_tensor_tensor(col(sc, DC), col(sc, MU), -X_UP, col(sc, RS), ALU.mult, ALU.mult))
                dve.wait_ge(spec_mm, n + 1)
                if has_prev:
                    dve.wait_ge(xturn_mm, n)
                    dve.wait_ge(xdiag_ready, 4 * n)
                nc.vector.tensor_scalar(xnorm[:, :, :, :].rearrange("p g n e -> p (g n e)"), bank[3][:, 0:P],
                                        col(sc, XS), None, ALU.mult).then_inc(spec_read, 1)
                dve.wait_ge(spec_read, n + 1)
                then(nc.vector.tensor_tensor(xnorm[0:32, 0, 0, 1:2], xnorm[0:32, 0, 0, 1:2], sc[0:32, DC:DC + 1], ALU.add))
                xn = xnorm[:, :, :, :].rearrange("p g n e -> p n g e")
                then(nc.vector.tensor_copy(xtri[:, :, 0, :, 0:2], xn))
                then(nc.vector.tensor_tensor(xtri[:, :, 1, :, 0:2], xn, xtri[:, :, 0, :, 0:2], ALU.subtract))
                tri = xtri[:, :, :, :, :].rearrange("p n h g e -> p (n h g) e")
                nc.vector.tensor_scalar(tri[:, :, 2], tri[:, :, 0], -1.0, None, ALU.mult).then_inc(xtri_ready, 1)
                if has_prev:
                    conv_add(n - 1, 1 - k, 4)
                    conv_add(n - 1, 1 - k, 5)
                    conv_add(n - 1, 1 - k, 6)
                for ri in range(2):
                    dve.wait_ge(ostat_hi, 2 * n + ri + 1)
                    for s in range(4):
                        lo = ostat[64:P, :, :].rearrange("p o (g r s) -> p r s g o", g=4, r=2)[:, ri, s]
                        src = bank[ri][64:P, P * s:P * s + P].rearrange("p (g o) -> p g o", g=4)
                        last = nc.vector.scalar_tensor_tensor(lo, src, O_DOWN, lo, ALU.mult, ALU.subtract)
                then(last)
                nc.vector.tensor_copy(ostat[:, :, 4], bias_half[:, :]).then_inc(ostat_ready, 1)
                then(nc.vector.tensor_copy(ospec, bank[1][0:32, :]))
                dve.wait_ge(xturn_mm, n + 1)
                xt = bank[3][0:32, :].rearrange("p (g s c) -> p s g c", g=4, s=4)
                for s in range(4):
                    last = nc.vector.tensor_tensor(prod_ox[:, P * s:P * s + P].rearrange("p (g c) -> p g c", g=4), xt[:, s],
                                                   ospec[:, P * s:P * s + P].rearrange("p (g c) -> p g c", g=4), ALU.mult)
                then(last)
                then(nc.vector.tensor_tensor(prod_oo, ospec, ospec, ALU.mult))
                nc.vector.tensor_scalar(prod_oo[:, 0:C], prod_oo[:, 0:C], sel[:, P:P + 1], None, ALU.mult).then_inc(prods_ready, 1)
                dve.wait_ge(prods_ready, n + 1)
                if has_prev:
                    conv_add(n - 1, 1 - k, 7)
                    conv_add(n - 1, 1 - k, 8)
                dve.wait_ge(s2_mm, n + 1)
                mask16 = mask_g[:, :].unsqueeze(1).broadcast_to([P, 16, C])
                for src, to in ((bank[6], DOX), (bank[7], DOO)):
                    then(nc.vector.tensor_tensor_reduce(
                        out=junk.rearrange("p (k c) -> p k c", c=C), in0=src[:, :].rearrange("p (k c) -> p k c", c=C), in1=mask16,
                        scale=1.0, scalar=0.0, op0=ALU.mult, op1=ALU.add, accum_out=col(sc, to)))
                nc.vector.tensor_tensor_reduce(out=junk[:, 0:C], in0=bank[2][:, 128:128 + C], in1=mask_g[:, :],
                                               scale=1.0, scalar=0.0, op0=ALU.mult, op1=ALU.add,
                                               accum_out=col(sc, U0)).then_inc(s2_read, 1)

                def s2_scalars():
                    dve.wait_ge(s2_read, n + 1)
                    ve, rs, var0 = (col(sc, a + 1) for a in (VE, RS, VAR))
                    then(nc.vector.tensor_tensor(col(sc, SIG), ve, rs, ALU.mult))
                    then(nc.vector.tensor_tensor(col(sc, A0), col(sc, SIG), col(sc, DOX), ALU.mult))
                    then(nc.vector.scalar_tensor_tensor(col(sc, A0), col(sc, A0), col(nu, NUV), var0, ALU.mult, ALU.add))
                    then(nc.vector.tensor_tensor(col(sc, A1), col(sc, U0), col(sc, U0), ALU.mult))
                    then(nc.vector.tensor_tensor(col(sc, A1), col(sc, DOO), col(sc, A1), ALU.subtract))
                    then(nc.vector.scalar_tensor_tensor(col(sc, A0), col(sc, A1), col(nu, NUV2), col(sc, A0), ALU.mult, ALU.add))
                    nc.vector.tensor_scalar(col(sc, A0), col(sc, A0), 0.0, EPS, ALU.max, ALU.add).then_inc(var1_ready, 1)

                def s2_scalars_end():
                    rsqrt(A1, A0, 1, var1_ready, dev1_ready)
                    then(nc.vector.tensor_scalar(col(sc, GS), col(sc, A1), G_UP, None, ALU.mult))
                    then(nc.vector.scalar_tensor_tensor(col(sc, A2), col(sc, U0), col(nu, NUM), col(sc, MU + 1), ALU.mult, ALU.add))
                    then(nc.vector.tensor_tensor(col(sc, A2), col(sc, A2), col(nu, BIAS_CD), ALU.add))
                    nc.vector.scalar_tensor_tensor(col(sc, GB), col(sc, A2), -1.0, col(sc, GS), ALU.mult, ALU.mult)\
                        .then_inc(znorm_scalars, 1)

                def add_x(r):
                    for t in range(2):
                        v = 2 * r + t
                        dve.wait_ge(s_mm, 32 * n + v + 1)
                        part = img[k][:, t, 2 * r:2 * r + 2, :].rearrange("p c w -> p (c w)")
                        nc.vector.scalar_tensor_tensor(part, bank[4 + v % 4][:, :], col(nu, ALPHA), part, ALU.mult, ALU.add)\
                            .then_inc(x1_added, 1)

                for r in range(16):
                    dve.wait_ge(t_hi, 16 * n + r + 1)
                    lo = trow[r % 2][64:P, :]
                    nc.vector.scalar_tensor_tensor(lo, bank[r % 2][64:P, :], T_DOWN, lo, ALU.mult, ALU.subtract).then_inc(t_lo, 1)
                    if r == 2:
                        s2_scalars()
                    if r == 6:
                        s2_scalars_end()
                    if r >= 1:
                        add_x(r - 1)
                add_x(15)
                for v in range(10):
                    dve.wait_ge(g_hi, 10 * n + v + 1)
                    z, w, hi = corner(v, 0)
                    lo = corner(v, 1)[2]
                    nc.vector.tensor_tensor(lo, corner_in(z, v), hi, ALU.subtract).then_inc(g_lo, 1)
                assert at[0] == STEPS, at[0]

            STEPS = DVE_STEPS
            setup()
            over_samples(dve, step)
            for u in range(9):
                conv_add(LAST, 1, u)


O_SCALE_INV = 2.0 ** -15
DVE_STEPS = 37


def _tables():
    import numpy as np
    p = np.arange(P)
    m = np.arange(M)

    def halves(a):
        hi = a.astype(np.float16)
        return hi, (a - hi).astype(np.float16)

    h = np.arange(2)[None, :, None] * P + p[:, None, None]
    ang = 2 * np.pi * (h * m % H) / H
    cf = np.concatenate([np.cos(ang), np.sin(ang)], -1).astype(np.float32)
    ang = 2 * np.pi * (h * m % W) / W
    lt = np.zeros((P, 4, 96), np.float32)
    for half in range(2):
        c, s = np.cos(ang[:, half]), np.sin(ang[:, half])
        lt[:, half, 0:32:2], lt[:, half, 1:32:2] = -s, c
        lt[:, 2 + half, 0:32:2], lt[:, 2 + half, 1:32:2] = -c, -s
    w = np.arange(W)
    ang = 2 * np.pi * (m[:, None] * w % W) / W
    hi, lo = halves(np.stack([np.cos(ang), np.sin(ang)], 1).reshape(32, W))
    cst = np.concatenate([hi, lo, hi, lo], 0)
    g, r, s = np.meshgrid(np.arange(4), np.arange(2), np.arange(4), indexing="ij")
    mm = (4 * g + s).reshape(32, 1)
    rr = r.reshape(32, 1)
    hh = np.arange(H)
    ang = 2 * np.pi * (mm * hh % H) / H
    e = np.where(rr == 0, np.cos(ang), -np.sin(ang))
    e[4] = 1.0
    hi, lo = halves(e * E_UP)
    et = np.concatenate([hi, lo, hi, lo], 0).reshape(P, 2, P)
    c = np.arange(C)
    same_sc = (p[:, None] % C) // 2 == c // 2
    same_cd = (p[:, None] % C) // 2 == c // 2
    msc, mcd = (np.repeat(a[:, :, None] / 512.0, 2, 2).astype(np.float32) for a in (same_sc, same_cd))
    sel = np.zeros((32, 2 * P), np.float32)
    sel[1, :P] = 1
    sel[:, P] = 1
    sel[0, P], sel[1, P] = 0, 2
    return {"cf": cf, "lt": lt, "cst": cst, "et": et, "ident": np.eye(P, dtype=np.float32),
            "rep": (p % C == c[:, None]).astype(np.float32), "msc": msc, "mcd": mcd,
            "mg": same_cd.astype(np.float32), "dw": (p[:, None] // C == np.arange(4)).astype(np.float32), "sel": sel}


_INS = ["x", "L0_conv_w_real", "L0_conv_w_imag", "L1_conv_weight", "L1_conv_bias"]


def kernel(**inputs):
    import numpy as _np
    import concourse.bacc as _bacc
    from concourse import mybir as _mybir
    from concourse.bass_utils import run_bass_kernel_spmd as _run

    nc = _bacc.Bacc("TRN2", target_bir_lowering=False, num_devices=1)
    arrays, args = {}, []
    for name, a in [(n, inputs[n]) for n in _INS] + list(_tables().items()):
        a = _np.ascontiguousarray(a)
        arrays[f"in_{name}_dram"] = a
        args.append(nc.dram_tensor(f"in_{name}_dram", a.shape, _mybir.dt.from_np(a.dtype), kind="ExternalInput").ap())
    o = nc.dram_tensor("out_0_dram", (B, C, H, W), _mybir.dt.float32, kind="ExternalOutput").ap()
    bass_spectral_then_conv(nc, *args, o)
    r = _run(nc, [arrays], core_ids=[0])
    return r.results[0]["out_0_dram"]
```

```python
import concourse.bass as bass
from concourse import mybir
from contextlib import ExitStack

B, C, H, W = 16, 32, 256, 256
N = H * W
M = 16
P = 128
EPS = 1e-5
K3 = 3
FFT = 512
CUT = (FFT - H) // 2
OUTW = H + K3 - 1 - CUT
NBLK = 33
COL0 = W - 4 * NBLK
TAPW = 4 + K3 - 1
X_UP = 4096.0
W_UP = 1024.0
O_DOWN = 2.0 ** -13
T_DOWN = 2.0 ** -4
E_UP = 1024.0
G_UP = 64.0
K_UP = 1024.0


def bass_spectral_then_conv(nc: bass.Bass, x, w_real, w_imag, conv_w, conv_b,
                            cf_d, l_d, cst_d, e_d, ident_d, rep_d, m2_d, mg_d, dw_d, sel_d, out, samples=B):
    f32, f16 = mybir.dt.float32, mybir.dt.float16
    ALU, ACT, AX = mybir.AluOpType, mybir.ActivationFunctionType, mybir.AxisListType
    ctx = ExitStack()
    with ctx:
        def sb(name, shape, dt):
            return ctx.enter_context(nc.sbuf_tensor(name, shape, dt))

        def sem(name):
            return ctx.enter_context(nc.semaphore(name))

        img = [sb(f"img{k}", [P, 2, C, W], f32) for k in range(2)]
        wmix = sb("wmix", [P, 2, 2, M, P], f16)
        colsum = sb("colsum", [P, 2, 512], f32)
        shared = sb("shared", [P, 2048], f32)
        turned = shared[:, :].rearrange("p (h m c) -> p h m c", h=2, m=32)
        obroad = shared[:, 0:1024].rearrange("p (k c f) -> p k c f", k=8, c=4)
        prod_oo = shared[0:32, 512:1024]
        ospec = shared[0:32, 1024:1536]
        prod_ox = shared[0:32, 1536:2048]
        trow = [shared[:, 256 * k:256 * k + 256].bitcast(f16) for k in range(2)]
        stats = sb("stats", [P, C, 6], f32)
        moments = sb("moments", [P, 2, C, 2], f32)
        meansq = sb("meansq", [P, C, 2], f32)
        xnorm = sb("xnorm", [P, 4, M, 2], f32)
        xtri = sb("xtri", [P, M, 2, 4, 3], f16)
        xdiag = sb("xdiag", [P, M * 2, 4, 12], f16)
        opair = sb("opair", [P, 2, 4, M, 2], f32)
        ostat = sb("ostat", [P, C, 32], f16)
        half = sb("half", [P, 3, 512], f32)
        edge = sb("edge", [2, 2, 9 * P], f32)
        gn = sb("gn", [P, 2, NBLK, OUTW], f16)
        prod_sum = sb("prod_sum", [32, 2, C], f32)
        junk = sb("junk", [P, 3 * C], f32)
        edge_out = sb("edge_out", [NBLK, 2, P], f32)
        wconv = sb("wconv", [P, 2, K3, TAPW * C], f16)
        bias_rows = sb("bias_rows", [P, C], f32)
        bias_half = sb("bias_half", [P, C], f16)
        cf = sb("cf", [P, 2, 32], f32)
        lt = sb("lt", [P, 4, 96], f32)
        cst = sb("cst", [P, W], f16)
        et = sb("et", [P, 2, P], f16)
        ident = sb("ident", [P, P], f32)
        ones = sb("ones", [P, P], f32)
        rep = sb("rep", [C, P], f32)
        mask2 = sb("mask2", [P, C, 2], f32)
        mask_g = sb("mask_g", [P, C], f32)
        dw_is = sb("dw_is", [P, 4], f32)
        sel = sb("sel", [32, 2 * P], f32)
        nu = sb("nu", [P, 12], f32)
        sc = sb("sc", [P, 32], f32)
        bank = [ctx.enter_context(nc.psum_tensor(f"bank{k}", [P, 512], f32)) for k in range(8)]

        wflat = gn[:, :, :, :].rearrange("p a b c -> p (a b c)").bitcast(f32)[:, 0:2 * 2048]\
            .rearrange("p (r f) -> p r f", r=2)
        edge_rows = bank[2][:, 128:128 + 2 * NBLK]

        MAXES, NU0, RNU0, NU1, RNU1, ALPHA, BETA, NUV, NUV2, NUM, BIAS_CD = range(11)
        MU, MS, MUSQ, VAR, VE, RS, XS, DC, DOX, DOO, U0, SIG, A0, A1, A2, GS, GB, ROOT, ROOT2 = range(19)

        def col(t, k, n=1):
            return t[:, k:k + n]

        tables_in = sem("tables_in")
        weights_in = sem("weights_in")
        slot_in = [sem(f"slot_in{s}") for s in range(4)]
        bias_in = sem("bias_in")
        ones_set = sem("ones_set")
        peak_col = sem("peak_col")
        peak_row = sem("peak_row")
        peak_got = sem("peak_got")
        peak_all = sem("peak_all")
        nu_set = sem("nu_set")
        conv_rep = sem("conv_rep")
        mix_hi = sem("mix_hi")
        wconv_set = sem("wconv_set")
        weights_done = sem("weights_done")
        cleared = sem("cleared")
        loaded = [[sem(f"loaded{k}{q}") for q in range(4)] for k in range(2)]
        cols_mm = sem("cols_mm")
        cols_sb = sem("cols_sb")
        turn_mm = sem("turn_mm")
        turn_sb = sem("turn_sb")
        moments_ready = sem("moments_ready")
        sums_mm = sem("sums_mm")
        var_ready = sem("var_ready")
        dev_ready = sem("dev_ready")
        var1_ready = sem("var1_ready")
        dev1_ready = sem("dev1_ready")
        spec_mm = sem("spec_mm")
        spec_read = sem("spec_read")
        xtri_ready = sem("xtri_ready")
        xdiag_ready = sem("xdiag_ready")
        mix_mm = sem("mix_mm")
        obroad_ready = sem("obroad_ready")
        oturn_mm = sem("oturn_mm")
        xturn_mm = sem("xturn_mm")
        ostat_hi = sem("ostat_hi")
        ostat_ready = sem("ostat_ready")
        ospec_ready = sem("ospec_ready")
        xt_read = sem("xt_read")
        prods_ready = sem("prods_ready")
        s2_mm = sem("s2_mm")
        s2_read = sem("s2_read")
        znorm_scalars = sem("znorm_scalars")
        t_mm = sem("t_mm")
        t_hi = sem("t_hi")
        t_lo = sem("t_lo")
        s_mm = sem("s_mm")
        x1_up = sem("x1_up")
        s_copied = sem("s_copied")
        x1_low = sem("x1_low")
        packed = sem("packed")
        corner_mm = sem("corner_mm")
        edge_turned = sem("edge_turned")
        z_ready = sem("z_ready")
        g_hi = sem("g_hi")
        g_lo = sem("g_lo")
        edge_mm = sem("edge_mm")
        edge_sb = sem("edge_sb")
        edge_back = [sem(f"edge_back{k}") for k in range(2)]
        edge_added = sem("edge_added")
        edge_done = sem("edge_done")
        edge_stored = sem("edge_stored")
        conv_mm = sem("conv_mm")
        conv_added = sem("conv_added")
        stored = [[sem(f"stored{t}{q}") for q in range(4)] for t in range(2)]
        act_step = sem("act_step")
        dve_step = sem("dve_step")
        dve_setup = sem("dve_setup")
        pe_setup = sem("pe_setup")

        PIECES = [(u, j) for u in range(9) for j in range(4 * u, min(4 * u + 5, NBLK))]
        SLOTS = [6, 4, 4] + [4, 3, 2, 2] + [4] * 4 + [0] * 8
        S2_SLOT = 6
        assert sum(SLOTS) == len(PIECES) == 41

        S2_WAIT, ROOT_WAIT, ROOT_STEP = 6, 4, 6

        def pieces_in(slot):
            return PIECES[sum(SLOTS[:slot]):sum(SLOTS[:slot + 1])]

        def banks_ending_in(slot):
            return [u for u, j in pieces_in(slot) if j == min(4 * u + 4, NBLK - 1)]

        def conv_ps(u):
            return bank[4 + u % 2]

        EDGE_J = [(0, 8), (8, 16), (16, 24), (24, NBLK)]
        CORNER = [(4 * k, min(4 * k + 4, NBLK)) for k in range(9)]

        QS = (3, 2, 0, 1)
        xr = x.rearrange("b (q c) (t p) w -> b t q p c w", q=4, t=2)
        outr = out.rearrange("b (q c) (t p) w -> b t q p c w", q=4, t=2)
        LAST = samples - 1
        PAIRS = (samples - 2) // 2

        def over_samples(eng, step):
            step(0, 0, 0)
            if PAIRS:
                with eng.Fori(0, PAIRS) as p:
                    step(2 * p + 1, p, 1)
                    step(2 * p + 2, p + 1, 0)
            step(LAST, LAST // 2, 1)

        def corner(v, part):
            if v < 9:
                j0, j1 = CORNER[v]
                w = P * (j1 - j0)
                return half[:, v % 3, 0:w], w, gn[:, part, j0:j1, 2:OUTW]
            return half[:, v % 3, 0:2 * NBLK], 2 * NBLK, gn[:, part, :, 0:2]

        def corner_in(z, v):
            return z.rearrange("p (j h) -> p j h", h=P) if v < 9 else z.rearrange("p (j r) -> p j r", r=2)

        block = ctx.enter_context(nc.Block())

        @block.sync
        def _(sp):
            for ri, w in enumerate((w_real, w_imag)):
                sp.dma_start(wflat[:, ri, :], w.rearrange("i (a o) m n -> (i a) (o m n)", a=4))\
                    .then_inc(weights_in, 16)
            sp.dma_start(shared[0:C, 0:288].rearrange("c (o k) -> c o k", k=9),
                         conv_w.rearrange("o c a b -> c o (a b)")).then_inc(weights_in, 16)
            sp.dma_start(nu[0:C, BIAS_CD:BIAS_CD + 1], conv_b.rearrange("(c a) -> c a", a=1)).then_inc(weights_in, 16)
            for dst, src in ((cf, cf_d), (lt, l_d), (cst, cst_d), (et, e_d), (ident, ident_d), (rep, rep_d),
                             (mask2, m2_d), (mask_g, mg_d), (dw_is, dw_d), (sel, sel_d)):
                sp.dma_start(dst[:], src).then_inc(tables_in, 16)
            for s in range(4):
                for ri, w in enumerate((w_real, w_imag)):
                    sp.dma_start(img[1][32 * s:32 * s + 32, ri].rearrange("p c w -> p (c w)"),
                                 w.rearrange("i o m n -> i (o m n)")).then_inc(slot_in[s], 16)
            for q in QS:
                for t in range(2):
                    sp.dma_start(img[0][:, t, 8 * q:8 * q + 8, :], xr[0, t, q]).then_inc(loaded[0][q], 16)
            sp.wait_ge(weights_done, 1)
            for q in QS:
                for t in range(2):
                    sp.dma_start(img[1][:, t, 8 * q:8 * q + 8, :], xr[1, t, q]).then_inc(loaded[1][q], 16)

            def turn_over(n, k, load):
                def send(t, q, first=0):
                    sp.dma_start(outr[n - 1, t, q, first:P], img[1 - k][first:P, t, 8 * q:8 * q + 8, :])\
                        .then_inc(stored[t][q], 16)

                def fetch(t, q):
                    sp.dma_start(img[1 - k][:, t, 8 * q:8 * q + 8, :], xr[n + 1, t, q]).then_inc(loaded[1 - k][q], 16)

                sp.wait_ge(x1_low, 16 * n)
                for q in QS:
                    send(1, q, OUTW - CUT)
                sp.wait_ge(edge_done, n)
                sp.dma_start(out[n - 1, :, CUT:OUTW, :].rearrange("c h w -> h c w"), img[1 - k][0:OUTW - CUT, 1])\
                    .then_inc(edge_stored, 16)
                if load:
                    for q in QS:
                        sp.wait_ge(stored[1][q], 16 * n)
                    sp.wait_ge(edge_stored, 16 * n)
                    for q in QS:
                        fetch(1, q)
                sp.wait_ge(conv_added, 9 * n)
                for sends, fetches in (((3, 2), (3,)), ((0, 1), (2, 0)), ((), (1,))):
                    for q in sends:
                        send(0, q)
                    if load:
                        for q in fetches:
                            sp.wait_ge(stored[0][q], 16 * n)
                        for q in fetches:
                            fetch(0, q)

            if PAIRS:
                with sp.Fori(2, PAIRS + 2) as p:
                    turn_over(2 * p - 3, 1, True)
                    turn_over(2 * p - 2, 0, True)
            turn_over(LAST, 1, False)
            turn_over(samples, 0, False)
            for t in range(2):
                for q in range(4):
                    sp.wait_ge(stored[t][q], 16 * samples)
            sp.wait_ge(edge_stored, 16 * samples)

        @block.tensor
        def _(pe):
            def setup():
                pe.wait_ge(tables_in, 160)
                pe.wait_ge(peak_col, 2)
                nc.tensor.matmul(bank[0][0:1, 0:P], col(sc, 0), ident[:, :], start=True, stop=True)
                nc.tensor.matmul(bank[0][0:1, P:2 * P], col(sc, 1), ident[:, :], start=True, stop=True).then_inc(peak_row, 1)
                pe.wait_ge(ones_set, 1)
                pe.wait_ge(peak_got, 1)
                nc.tensor.matmul(bank[1][:, 0:2], ones[0:1, :], sc[0:1, 2:4], start=True, stop=True).then_inc(peak_all, 1)
                nc.tensor.matmul(bank[2][:, 0:288], rep[:, :], shared[0:C, 0:288], start=True, stop=True)
                nc.tensor.matmul(bank[3][:, 0:1], rep[:, :], nu[0:C, BIAS_CD:BIAS_CD + 1], start=True, stop=True)\
                    .then_inc(conv_rep, 1)

            def conv_edge(n):
                pe.wait_ge(g_lo, 10 * n + 10)
                for i in range(2):
                    pairs = [(OUTW - 1, 1), (OUTW - 2, 2)] if i == 0 else [(OUTW - 1, 2)]
                    terms = [(r, a, gh, wh) for r, a in pairs for gh, wh in ((0, 0), (0, 1), (1, 0))]
                    for k, (r, a, gh, wh) in enumerate(terms):
                        nc.tensor.matmul(bank[6][0:NBLK, i * P:i * P + 64], gn[:, gh, :, r],
                                         wconv[:, wh, a, 4 * C:6 * C], start=(k == 0), stop=False, skip_group_check=True)
                        last = nc.tensor.matmul(bank[6][0:NBLK - 1, i * P:i * P + P], gn[:, gh, 1:NBLK, r],
                                                wconv[:, wh, a, 0:4 * C], start=False, stop=(k == len(terms) - 1),
                                                skip_group_check=True)
                last.then_inc(edge_mm, 1)

            def conv_piece(n, u, j):
                if u == 0 and j == 0:
                    pe.wait_ge(g_lo, 10 * n + 10)
                if j == 4 * u and u >= 2:
                    pe.wait_ge(conv_added, 9 * n + u - 1)
                lo = 0 if j > 4 * u else 4
                hi = TAPW if j < 4 * u + 4 else 4
                at = (j - 1 - 4 * u + (1 if lo else 0)) * P
                jobs = [(a, gh, wh) for gh, wh in ((0, 0), (0, 1), (1, 0)) for a in range(K3)]
                ends = j == min(4 * u + 4, NBLK - 1)
                for k, (a, gh, wh) in enumerate(jobs):
                    last = nc.tensor.matmul(conv_ps(u)[:, at:at + (hi - lo) * C], gn[:, gh, j, 2 - a:2 - a + P],
                                            wconv[:, wh, a, lo * C:hi * C], start=(j == 4 * u and k == 0),
                                            stop=(ends and k == len(jobs) - 1), skip_group_check=True)
                if ends:
                    last.then_inc(conv_mm, 1)

            def corner_turn(n, v):
                if v == 0:
                    pe.wait_ge(x1_up, 16 * n + 16)
                    pe.wait_ge(s_copied, 16 * n + 16)
                if v >= 2:
                    pe.wait_ge(z_ready, 10 * n + v - 1)
                pe.wait_ge(packed, 9 * n + v + 1)
                for j in range(CORNER[v][1] - CORNER[v][0]):
                    last = nc.tensor.transpose(bank[6 + v % 2][:, P * j:P * j + P], half[:, v % 3, P * j:P * j + P], ident[:, :])
                last.then_inc(corner_mm, 1)

            def edge_turn(n, k, i):
                for j in range(NBLK * i // 4, NBLK * (i + 1) // 4):
                    for d in range(4):
                        last = nc.tensor.matmul(edge_rows[32 * d:32 * d + 32, 2 * j:2 * j + 2],
                                                img[k][96:P, 0, :, COL0 + 4 * j + d], ident[96:P, P - 2:P],
                                                start=True, stop=True)
                last.then_inc(edge_turned, 1)

            def conv_slot(n, slot):
                for u, j in pieces_in(slot):
                    if (u, j) == (5, 20):
                        pe.wait_ge(s2_read, n + 2)
                    conv_piece(n, u, j)

            def step(n, use, k):
                prev = n - 1
                has_prev = not isinstance(n, int) or n > 0
                if has_prev:
                    pe.wait_ge(t_lo, 16 * n)
                for i, q in enumerate(QS):
                    pe.wait_ge(loaded[k][q], 32 * (use + 1))
                    if i > 0 or has_prev:
                        pe.wait_ge(cols_sb, 4 * n + i)
                    for t in range(2):
                        for j in range(4):
                            last = nc.tensor.matmul(
                                bank[0][32 * j:32 * j + 32, :], cf[:, t, :],
                                img[k][:, t, 8 * q + j:8 * q + j + 5:4, :], start=(t == 0), stop=(t == 1))
                    last.then_inc(cols_mm, 1)
                    if has_prev:
                        corner_turn(prev, 2 * i)
                    pe.wait_ge(cols_sb, 4 * n + i + 1)
                    if i > 0 or has_prev:
                        pe.wait_ge(turn_sb, 4 * n + i)
                    for e in range(2):
                        for h in range(2):
                            last = nc.tensor.transpose(bank[1][:, (h * 2 + e) * P:(h * 2 + e + 1) * P],
                                                       colsum[:, i % 2, e * W + h * P:e * W + h * P + P], ident[:, :])
                    last.then_inc(turn_mm, 1)
                    if has_prev:
                        edge_turn(prev, 1 - k, i)
                        corner_turn(prev, 2 * i + 1)
                pe.wait_ge(moments_ready, n + 1)
                nc.tensor.matmul(bank[2][:, 0:P], ones[:, :], moments[:, :, :, :], start=True, stop=True).then_inc(sums_mm, 1)
                if has_prev:
                    corner_turn(prev, 8)
                pe.wait_ge(turn_sb, 4 * n + 4)
                for g in range(4):
                    for k4 in range(4):
                        ab, h = k4 // 2, k4 % 2
                        last = nc.tensor.matmul(bank[3][:, 32 * g:32 * g + 96],
                                                turned[:, h, 16 * ab + 4 * g:16 * ab + 4 * g + 4, :],
                                                lt[:, k4, :], start=(k4 == 0), stop=(k4 == 3))
                last.then_inc(spec_mm, 1)
                if has_prev:
                    conv_edge(prev)
                    conv_slot(prev, 0)
                pe.wait_ge(xdiag_ready, 4 * n + 4)
                pe.wait_ge(spec_read, n + 1)
                for m in range(M):
                    terms = [(ri, wh, xh) for wh, xh in ((0, 0), (0, 1), (1, 0)) for ri in range(2)]
                    for t, (ri, wh, xh) in enumerate(terms):
                        rhs = xdiag[:, 2 * m + xh].rearrange("p s (g e) -> p (s g) e", e=3)[:, :, ri:ri + 2]
                        last = nc.tensor.matmul(bank[3][:, 32 * m:32 * m + 32], wmix[:, wh, ri, m, :], rhs,
                                                start=(t == 0), stop=(t == len(terms) - 1))
                last.then_inc(mix_mm, 1)
                if has_prev:
                    conv_slot(prev, 1)
                pe.wait_ge(obroad_ready, n + 1)
                for ri in range(2):
                    for s in range(4):
                        last = nc.tensor.transpose(bank[ri][:, P * s:P * s + P],
                                                   obroad[:, 4 * ri + s].rearrange("p c f -> p (c f)"), ident[:, :])
                last.then_inc(oturn_mm, 1)
                for g in range(4):
                    last = nc.tensor.transpose(bank[7][0:32, P * g:P * g + P], xnorm[:, g], ident[:, :])
                last.then_inc(xturn_mm, 1)
                if has_prev:
                    conv_slot(prev, 2)
                pe.wait_ge(ostat_ready, n + 1)

                def over_w(r):
                    if r == 1:
                        pe.wait_ge(ospec_ready, n + 1)
                    for o in range(2):
                        for c in range(4):
                            last = nc.tensor.matmul(bank[r % 2][32 * c:32 * c + 32, o * W:o * W + W],
                                                    ostat[:, 2 * r + o, :], cst[:, :], start=True, stop=True)
                    last.then_inc(t_mm, 1)

                over_w(0)
                over_w(1)
                for r in range(16):
                    pe.wait_ge(t_lo, 16 * n + r + 1)
                    if r == 0 and has_prev:
                        pe.wait_ge(edge_sb, n)
                    for t in range(2):
                        if r >= 2:
                            pe.wait_ge((x1_up, s_copied)[t], 16 * n + r - 1)
                        if r == 1 and t == 1:
                            pe.wait_ge(xt_read, n + 1)
                        nc.tensor.matmul(bank[2 + 4 * (r % 2) + t][:, :], et[:, t, :], trow[r % 2], start=True, stop=True)\
                            .then_inc(s_mm, 1)
                    if r < 14:
                        over_w(r + 2)
                    if r + 3 == S2_SLOT:
                        pe.wait_ge(prods_ready, n + 1)
                        if has_prev:
                            pe.wait_ge(conv_added, 9 * prev + 4)
                        nc.tensor.matmul(bank[5][:, 0:2 * C], ones[0:32, :], prod_sum[:, :, :], start=True, stop=True)
                        nc.tensor.matmul(bank[5][:, 2 * C:3 * C], sel[:, 0:P], ospec[:, 0:C], start=True, stop=True)\
                            .then_inc(s2_mm, 1)
                    if has_prev:
                        conv_slot(prev, 3 + r)

            setup()
            over_samples(pe, step)
            pe.wait_ge(x1_up, 16 * samples)
            pe.wait_ge(s_copied, 16 * samples)
            for v in range(9):
                corner_turn(LAST, v)
                if v < 4:
                    edge_turn(LAST, 1, v)
            conv_edge(LAST)
            pe.wait_ge(conv_added, 9 * LAST)
            for u, j in PIECES:
                conv_piece(LAST, u, j)

        @block.scalar
        def _(act):
            def edge_out_copy(n):
                act.wait_ge(edge_mm, n + 1)
                src = bank[6][:, 0:2 * P].rearrange("p (i f) -> p i f", i=2)
                nc.scalar.activation(edge_out[0:32, :, :], src[0:32], ACT.Copy, scale=nu[0:32, BETA:BETA + 1])
                nc.scalar.activation(edge_out[32:33, :, 0:64], src[32:33, :, 0:64], ACT.Copy,
                                     scale=nu[32:33, BETA:BETA + 1]).then_inc(edge_sb, 1)
                act.wait_ge(edge_sb, n + 1)

            def edge_out_send(n, first):
                for q in (first, first + 1):
                    j0, j1 = EDGE_J[q]
                    if q >= 2:
                        act.wait_ge(edge_added, 3 * n + q - 1)
                    for i in range(2):
                        act.dma_start(edge[i:i + 1, q % 2, 0:P * (j1 - j0)].rearrange("p (j f) -> p j f", f=P),
                                      edge_out[j0:j1, i, :]).then_inc(edge_back[q % 2], 16)

            act.wait_ge(nu_set, 1)
            for s in range(4):
                act.wait_ge(slot_in[s], 32)
                rows = slice(32 * s, 32 * s + 32)
                for ri in range(2):
                    src = img[1][rows, ri].rearrange("p c w -> p (c w)").rearrange("p (o g s n) -> p s n g o", o=C, g=4, s=4)[:, s]
                    dst = wmix[rows, 0, ri].rearrange("p n (g o) -> p n g o", g=4)
                    nc.scalar.activation(dst, src, ACT.Copy, scale=nu[rows, RNU0:RNU0 + 1]).then_inc(mix_hi, 1)

            def pack(n, k, v):
                if v == 0:
                    act.wait_ge(x1_low, 16 * n + 16)
                if v >= 3:
                    act.wait_ge(g_lo, 10 * n + v - 2)
                j0, j1 = CORNER[v]
                src = img[k][:, 1, :, COL0 + 4 * j0:COL0 + 4 * j1].rearrange("p c w -> p w c")
                nc.scalar.activation(half[:, v % 3, 0:P * (j1 - j0)].rearrange("p (w c) -> p w c", c=C), src, ACT.Copy)\
                    .then_inc(packed, 1)

            def normalise(n, v):
                if v < 9:
                    act.wait_ge(corner_mm, 9 * n + v + 1)
                else:
                    act.wait_ge(edge_turned, 4 * n + 4)
                if v == 0:
                    act.wait_ge(znorm_scalars, n + 1)
                if v == 9:
                    act.wait_ge(g_lo, 10 * n + v - 2)
                z, w, dst = corner(v, 0)
                src = bank[6 + v % 2][:, 0:w] if v < 9 else edge_rows
                nc.scalar.activation(z, src, ACT.Identity, bias=col(sc, GB), scale=col(sc, GS))\
                    .then_inc(z_ready, 1)
                act.wait_ge(z_ready, 10 * n + v + 1)
                nc.scalar.activation(dst, corner_in(z, v), ACT.Copy).then_inc(g_hi, 1)

            def step(n, use, k):
                has_prev = not isinstance(n, int) or n > 0
                if has_prev:
                    pack(n - 1, 1 - k, 0)
                    pack(n - 1, 1 - k, 1)
                for i, q in enumerate(QS):
                    act.wait_ge(cols_mm, 4 * n + i + 1)
                    if i >= 2:
                        act.wait_ge(turn_mm, 4 * n + i - 1)
                    elif has_prev:
                        act.wait_ge(turn_mm, 4 * n)
                    nc.scalar.activation(colsum[:, i % 2, :], bank[0][:, :], ACT.Copy).then_inc(cols_sb, 1)
                    if has_prev:
                        normalise(n - 1, 2 * i)
                        pack(n - 1, 1 - k, 2 * i + 2)
                    act.wait_ge(turn_mm, 4 * n + i + 1)
                    if i == 0 and not has_prev:
                        act.wait_ge(wconv_set, 1)
                    dst = turned[:, :, :, 8 * q:8 * q + 8].rearrange("p h m c -> p h c m")
                    nc.scalar.activation(dst, bank[1][:, :].rearrange("p (h c m) -> p h c m", h=2, c=8),
                                         ACT.Copy).then_inc(turn_sb, 1)
                    if has_prev:
                        normalise(n - 1, 2 * i + 1)
                        if i < 3:
                            pack(n - 1, 1 - k, 2 * i + 3)
                if has_prev:
                    normalise(n - 1, 8)
                act.wait_ge(var_ready, n + 1)
                nc.scalar.activation(col(sc, ROOT), col(sc, VE), ACT.Sqrt).then_inc(dev_ready, 1)
                if has_prev:
                    normalise(n - 1, 9)
                act.wait_ge(xtri_ready, n + 1)
                if has_prev:
                    act.wait_ge(mix_mm, n)
                for s in range(4):
                    rows = slice(32 * s, 32 * s + 32)
                    nc.scalar.activation(xdiag[rows, :, s, :], xtri[rows].rearrange("p n h g e -> p (n h) (g e)"),
                                         ACT.Copy).then_inc(xdiag_ready, 1)
                if has_prev:
                    edge_out_copy(n - 1)
                    edge_out_send(n - 1, 0)
                act.wait_ge(mix_mm, n + 1)
                for g in range(4):
                    rows = slice(32 * g, 32 * g + 32)
                    src = bank[3][rows, :].rearrange("p (n s g e) -> p g s n e", n=M, s=4, g=4)[:, g]
                    nc.scalar.activation(opair[rows, 1], src, ACT.Copy).then_inc(act_step, 1)
                act.wait_ge(act_step, 6 * n + 4)
                pairs = opair[:, :, :, :, :].rearrange("p r s n e -> p r (s n) e")
                nc.scalar.activation(pairs[:, 0, :, 0], pairs[:, 1, :, 1], ACT.Copy).then_inc(act_step, 1)
                nc.scalar.activation(pairs[:, 0, :, 1], pairs[:, 1, :, 0], ACT.Copy, scale=-1.0).then_inc(act_step, 1)
                act.wait_ge(act_step, 6 * n + 6)
                src = opair[:, :, :, :, :].rearrange("p r s n e -> p (r s) (n e)").unsqueeze(2).broadcast_to([P, 8, 4, 32])
                nc.scalar.activation(obroad, src, ACT.Copy).then_inc(obroad_ready, 1)
                if has_prev:
                    edge_out_send(n - 1, 2)
                act.wait_ge(oturn_mm, n + 1)
                for ri in range(2):
                    dst = ostat[:, :, :].rearrange("p o (g r s) -> p r s g o", g=4, r=2)[:, ri]
                    nc.scalar.activation(dst, bank[ri][:, :].rearrange("p (s g o) -> p s g o", s=4, g=4),
                                         ACT.Copy, scale=O_DOWN).then_inc(ostat_hi, 1)
                nc.scalar.activation(ospec, bank[1][0:32, :], ACT.Copy).then_inc(ospec_ready, 1)
                def rows_hi(r):
                    act.wait_ge(t_mm, 16 * n + r + 1)
                    nc.scalar.activation(trow[r % 2], bank[r % 2][:, :], ACT.Copy, scale=T_DOWN).then_inc(t_hi, 1)

                rows_hi(0)
                for r in range(16):
                    if r < 15:
                        rows_hi(r + 1)
                    act.wait_ge(s_mm, 32 * n + 2 * r + 2)
                    if r >= 2:
                        act.wait_ge(x1_low, 16 * n + r - 1)
                    nc.scalar.activation(half[:, r % 2, :], bank[3 + 4 * (r % 2)][:, :], ACT.Copy,
                                         scale=col(nu, ALPHA)).then_inc(s_copied, 1)
                    if r == ROOT_STEP:
                        act.wait_ge(var1_ready, n + 1)
                        nc.scalar.activation(col(sc, ROOT), col(sc, A0), ACT.Sqrt).then_inc(dev1_ready, 1)
                if has_prev:
                    act.wait_ge(edge_done, n)

            over_samples(act, step)
            pack(LAST, 1, 0)
            pack(LAST, 1, 1)
            for v in range(10):
                normalise(LAST, v)
                if v < 7:
                    pack(LAST, 1, v + 2)
            edge_out_copy(LAST)
            edge_out_send(LAST, 0)
            edge_out_send(LAST, 2)

        @block.gpsimd
        def _(pool):
            nc.gpsimd.memset(xdiag[:, :, :, :], 0.0).then_inc(cleared, 1)
            nc.gpsimd.memset(edge_out[:, :, :], 0.0).then_inc(cleared, 1)
            nc.gpsimd.memset(bias_rows[:, :], 0.0).then_inc(cleared, 1)
            pool.wait_ge(cleared, 3)
            for c in range(4):
                pool.dma_start(bias_rows[32 * c:32 * c + 1, :], conv_b.rearrange("(a c) -> a c", a=1)).then_inc(bias_in, 16)

            def edge_add(n, k):
                for q, (j0, j1) in enumerate(EDGE_J):
                    w0, w1 = 4 * j0, min(4 * j1, OUTW)
                    pool.wait_ge(edge_back[q % 2], 64 * n + 32 * (q // 2) + 32)
                    rows = img[k][0:2, 1, :, w0:w1]
                    src = edge[0:2, q % 2, 0:C * (w1 - w0)].rearrange("p (w o) -> p o w", o=C)
                    nc.gpsimd.tensor_tensor(rows, rows, src, ALU.add).then_inc(edge_added if q < 3 else edge_done, 1)

            def low_half(n, v):
                pool.wait_ge(g_hi, 10 * n + v + 1)
                z, w, hi = corner(v, 0)
                nc.gpsimd.tensor_tensor(corner(v, 1)[2], corner_in(z, v), hi, ALU.subtract).then_inc(g_lo, 1)

            def step(n, use, k):
                if not isinstance(n, int) or n > 0:
                    for v in range(10):
                        low_half(n - 1, v)
                    edge_add(n - 1, 1 - k)
                for r in range(16):
                    pool.wait_ge(s_copied, 16 * n + r + 1)
                    part = img[k][:, 1, 2 * r:2 * r + 2, :].rearrange("p c w -> p (c w)")
                    nc.gpsimd.tensor_tensor(part, part, half[:, r % 2, :], ALU.add).then_inc(x1_low, 1)

            over_samples(pool, step)
            for v in range(10):
                low_half(LAST, v)
            edge_add(LAST, 1)

        @block.vector
        def _(dve):
            nc.vector.memset(ones[:, :], 1.0).then_inc(ones_set, 1)
            count = [0]

            def link(ins):
                count[0] += 1
                ins.then_inc(dve_setup, 1)
                dve.wait_ge(dve_setup, count[0])

            def setup():
                dve.wait_ge(weights_in, 64)
                nc.vector.tensor_reduce(col(sc, 4), wflat.rearrange("p r f -> p (r f)"), AX.X, ALU.max).then_inc(dve_setup, 1)
                nc.vector.tensor_reduce(col(sc, 5), wflat.rearrange("p r f -> p (r f)"), AX.X, ALU.min).then_inc(dve_setup, 1)
                nc.vector.memset(col(sc, 6, 4), 0.0).then_inc(dve_setup, 1)
                count[0] += 3
                dve.wait_ge(dve_setup, 3)
                link(nc.vector.tensor_reduce(sc[0:C, 6:7], shared[0:C, 0:288], AX.X, ALU.max))
                link(nc.vector.tensor_reduce(sc[0:C, 7:8], shared[0:C, 0:288], AX.X, ALU.min))
                link(nc.vector.tensor_reduce(sc[0:C, 8:9], nu[0:C, BIAS_CD:BIAS_CD + 1], AX.X, ALU.max))
                nc.vector.scalar_tensor_tensor(col(sc, 1), col(sc, 7), -1.0, col(sc, 6), ALU.mult, ALU.max).then_inc(peak_col, 1)
                link(nc.vector.scalar_tensor_tensor(col(sc, 5), col(sc, 5), -1.0, col(sc, 4), ALU.mult, ALU.max))
                link(nc.vector.scalar_tensor_tensor(col(sc, 9), col(sc, 8), -1.0, col(sc, 8), ALU.mult, ALU.max))
                nc.vector.scalar_tensor_tensor(col(sc, 0), col(sc, 9), 1.0 / 64, col(sc, 5), ALU.mult, ALU.max).then_inc(peak_col, 1)
                dve.wait_ge(peak_row, 1)
                nc.vector.tensor_reduce(sc[0:1, 2:4], bank[0][0:1, 0:2 * P].rearrange("p (k f) -> p k f", k=2), AX.X, ALU.max)\
                    .then_inc(peak_got, 1)
                dve.wait_ge(peak_all, 1)
                link(nc.vector.tensor_scalar(nu[:, NU0:NU0 + 3:2], bank[1][:, 0:2], 1e-30, None, ALU.max))
                link(nc.vector.reciprocal(col(sc, 6), col(nu, NU0)))
                link(nc.vector.reciprocal(col(sc, 7), col(nu, NU1)))
                link(nc.vector.tensor_scalar(col(nu, RNU0), col(sc, 6), W_UP, None, ALU.mult))
                link(nc.vector.tensor_scalar(col(nu, RNU1), col(sc, 7), K_UP, None, ALU.mult))
                nc.vector.tensor_scalar(col(nu, ALPHA), col(nu, NU0), O_SCALE_INV, None, ALU.mult)
                link(nc.vector.tensor_scalar(col(nu, BETA), col(nu, NU1), 1.0 / (FFT * G_UP * K_UP), None, ALU.mult))
                nc.vector.tensor_scalar(col(nu, NUV), col(nu, NU0), 2.0 ** -34, None, ALU.mult)
                link(nc.vector.tensor_scalar(col(nu, NUM), col(nu, NU0), 2.0 ** -23, None, ALU.mult))
                link(nc.vector.tensor_tensor(col(nu, NUV2), col(nu, NUM), col(nu, NUM), ALU.mult))
                dve.wait_ge(conv_rep, 1)
                dve.wait_ge(tables_in, 160)
                nc.vector.tensor_copy(col(nu, BIAS_CD), bank[3][:, 0:1]).then_inc(nu_set, 1)
                taps = shared[:, 0:288].rearrange("p (a b o) -> p a b o", a=3, b=3)
                wide = shared[:, 512:512 + K3 * TAPW * C].rearrange("p (a f) -> p a f", a=3)
                link(nc.vector.tensor_scalar(taps, bank[2][:, 0:288].rearrange("p (o a b) -> p a b o", a=3, b=3),
                                             col(nu, RNU1), None, ALU.mult))
                link(nc.vector.memset(wide, 0.0))
                for d in range(4):
                    for a in range(K3):
                        part = wide[:, a, d * C:(d + 3) * C]
                        link(nc.vector.scalar_tensor_tensor(part, taps[:, a].rearrange("p b o -> p (b o)"),
                                                            col(dw_is, d), part, ALU.mult, ALU.add))
                link(nc.vector.tensor_copy(wconv[:, 0], wide))
                nc.vector.tensor_tensor(wconv[:, 1], wide, wconv[:, 0], ALU.subtract).then_inc(wconv_set, 1)
                dve.wait_ge(bias_in, 64)
                link(nc.vector.tensor_scalar(bias_rows[:, :], bias_rows[:, :], col(nu, RNU0), 2.0 ** 9 / W_UP, ALU.mult, ALU.mult))
                link(nc.vector.tensor_copy(bias_half[:, :], bias_rows[:, :]))
                link(nc.vector.tensor_tensor(bias_half[64:P, :], bias_rows[64:P, :], bias_half[64:P, :], ALU.subtract))
                for s in range(4):
                    rows = slice(32 * s, 32 * s + 32)
                    for ri in range(2):
                        dve.wait_ge(mix_hi, 2 * s + ri + 1)
                        for g in range(4):
                            src = img[1][rows, ri].rearrange("p c w -> p (c w)")\
                                .rearrange("p (o g s n) -> p g s n o", o=C, g=4, s=4)[:, g, s]
                            hi, lo = (wmix[rows, h, ri].rearrange("p n (g o) -> p g n o", g=4)[:, g] for h in range(2))
                            last = nc.vector.scalar_tensor_tensor(lo, src, nu[rows, RNU0:RNU0 + 1], hi, ALU.mult, ALU.subtract)
                last.then_inc(weights_done, 1)
                dve.wait_ge(cleared, 3)

            def conv_add(n, k, u):
                dve.wait_ge(conv_mm, 9 * n + u + 1)
                if u == 0:
                    dve.wait_ge(edge_turned, 4 * n + 4)
                w = min(16, OUTW - 16 * u)
                x1 = img[k][:, 0, :, 16 * u:16 * u + w]
                ps = conv_ps(u)[:, 0:w * C].rearrange("p (w o) -> p o w", o=C)
                nc.vector.scalar_tensor_tensor(x1, ps, col(nu, BETA), x1, ALU.mult, ALU.add).then_inc(conv_added, 1)

            def step(n, use, k):
                has_prev = not isinstance(n, int) or n > 0
                at = [0]

                def conv_adds(slot):
                    if has_prev:
                        for u in banks_ending_in(slot):
                            conv_add(n - 1, 1 - k, u)

                def then(ins):
                    at[0] += 1
                    ins.then_inc(dve_step, 1)
                    dve.wait_ge(dve_step, STEPS * n + at[0])

                def rsqrt(to, v, asked, root):
                    dve.wait_ge(asked, n + 1)
                    dve.wait_ge(root, n + 1)
                    then(nc.vector.reciprocal(col(sc, to), col(sc, ROOT)))
                    then(nc.vector.tensor_tensor(col(sc, ROOT2), col(sc, to), col(sc, to), ALU.mult))
                    then(nc.vector.tensor_tensor(col(sc, ROOT2), col(sc, ROOT2), col(sc, v), ALU.mult))
                    then(nc.vector.tensor_scalar(col(sc, ROOT2), col(sc, ROOT2), -0.5, 1.5, ALU.mult, ALU.add))
                    then(nc.vector.tensor_tensor(col(sc, to), col(sc, to), col(sc, ROOT2), ALU.mult))

                for i, q in enumerate(QS):
                    dve.wait_ge(loaded[k][q], 32 * (use + 1))
                    for c in range(8 * q, 8 * q + 8):
                        last = nc.vector.bn_stats(stats[:, c, :], img[k][:, :, c, :])
                then(last)
                mean, var = stats[:, :, 1:5:3], stats[:, :, 2:6:3]
                then(nc.vector.tensor_tensor(meansq[:, :, :], mean, mean, ALU.mult))
                if has_prev:
                    dve.wait_ge(sums_mm, n)
                nc.vector.tensor_copy(moments[:, 0], mean)
                nc.vector.scalar_tensor_tensor(moments[:, 1], var, 1.0 / 256, meansq[:, :, :], ALU.mult, ALU.add)\
                    .then_inc(moments_ready, 1)
                dve.wait_ge(moments_ready, n + 1)
                dve.wait_ge(sums_mm, n + 1)
                for kind, to in ((0, MU), (1, MS)):
                    then(nc.vector.tensor_tensor_reduce(
                        out=meansq[:, :, :].rearrange("p c e -> p (c e)"), in0=bank[2][:, 64 * kind:64 * kind + 64],
                        in1=mask2[:, :, :].rearrange("p c e -> p (c e)"), scale=1.0, scalar=0.0,
                        op0=ALU.mult, op1=ALU.add, accum_out=col(sc, to)))
                then(nc.vector.tensor_tensor(col(sc, MUSQ), col(sc, MU), col(sc, MU), ALU.mult))
                then(nc.vector.tensor_tensor(col(sc, VAR), col(sc, MS), col(sc, MUSQ), ALU.subtract))
                nc.vector.tensor_scalar(col(sc, VE), col(sc, VAR), 0.0, EPS, ALU.max, ALU.add).then_inc(var_ready, 1)
                rsqrt(RS, VE, var_ready, dev_ready)
                nc.vector.tensor_scalar(col(sc, XS), col(sc, RS), X_UP / N, None, ALU.mult)
                then(nc.vector.scalar_tensor_tensor(col(sc, DC), col(sc, MU), -X_UP, col(sc, RS), ALU.mult, ALU.mult))
                dve.wait_ge(spec_mm, n + 1)
                if has_prev:
                    dve.wait_ge(xturn_mm, n)
                    dve.wait_ge(xdiag_ready, 4 * n)
                nc.vector.tensor_scalar(xnorm[:, :, :, :].rearrange("p g n e -> p (g n e)"), bank[3][:, 0:P],
                                        col(sc, XS), None, ALU.mult).then_inc(spec_read, 1)
                dve.wait_ge(spec_read, n + 1)
                then(nc.vector.tensor_tensor(xnorm[0:32, 0, 0, 1:2], xnorm[0:32, 0, 0, 1:2], sc[0:32, DC:DC + 1], ALU.add))
                xn = xnorm[:, :, :, :].rearrange("p g n e -> p n g e")
                then(nc.vector.tensor_copy(xtri[:, :, 0, :, 0:2], xn))
                then(nc.vector.tensor_tensor(xtri[:, :, 1, :, 0:2], xn, xtri[:, :, 0, :, 0:2], ALU.subtract))
                tri = xtri[:, :, :, :, :].rearrange("p n h g e -> p (n h g) e")
                nc.vector.tensor_scalar(tri[:, :, 2], tri[:, :, 0], -1.0, None, ALU.mult).then_inc(xtri_ready, 1)
                conv_adds(0)
                conv_adds(1)
                for ri in range(2):
                    dve.wait_ge(ostat_hi, 2 * n + ri + 1)
                    for s in range(4):
                        lo = ostat[64:P, :, :].rearrange("p o (g r s) -> p r s g o", g=4, r=2)[:, ri, s]
                        src = bank[ri][64:P, P * s:P * s + P].rearrange("p (g o) -> p g o", g=4)
                        last = nc.vector.scalar_tensor_tensor(lo, src, O_DOWN, lo, ALU.mult, ALU.subtract)
                then(last)
                nc.vector.tensor_copy(ostat[:, :, 4], bias_half[:, :]).then_inc(ostat_ready, 1)
                dve.wait_ge(xturn_mm, n + 1)
                dve.wait_ge(ospec_ready, n + 1)
                xt = bank[7][0:32, :].rearrange("p (g s c) -> p s g c", g=4, s=4)
                for s in range(4):
                    last = nc.vector.tensor_tensor(prod_ox[:, P * s:P * s + P].rearrange("p (g c) -> p g c", g=4), xt[:, s],
                                                   ospec[:, P * s:P * s + P].rearrange("p (g c) -> p g c", g=4), ALU.mult)
                last.then_inc(xt_read, 1)

                def s2():
                    def step_done(ins):
                        at[0] += 1
                        ins.then_inc(dve_step, 1)

                    def previous_step():
                        dve.wait_ge(dve_step, STEPS * n + at[0])

                    step_done(nc.vector.tensor_tensor(prod_oo, ospec, ospec, ALU.mult))
                    yield
                    previous_step()
                    step_done(nc.vector.tensor_scalar(prod_oo[:, 0:C], prod_oo[:, 0:C], sel[:, P:P + 1], None, ALU.mult))
                    dve.wait_ge(xt_read, n + 1)
                    nc.vector.tensor_reduce(prod_sum[:, 0, :], prod_ox.rearrange("p (k c) -> p c k", c=C), AX.X, ALU.add)
                    yield
                    previous_step()
                    nc.vector.tensor_reduce(prod_sum[:, 1, :], prod_oo.rearrange("p (k c) -> p c k", c=C), AX.X, ALU.add)\
                        .then_inc(prods_ready, 1)
                    for _ in range(S2_WAIT):
                        yield
                    dve.wait_ge(s2_mm, n + 1)
                    for i, to in enumerate((DOX, DOO, U0)):
                        step_done(nc.vector.tensor_tensor_reduce(
                            out=junk[:, i * C:i * C + C], in0=bank[5][:, C * i:C * i + C], in1=mask_g[:, :],
                            scale=1.0, scalar=0.0, op0=ALU.mult, op1=ALU.add, accum_out=col(sc, to)))
                    nc.vector.tensor_tensor(col(sc, SIG), col(sc, VE), col(sc, RS), ALU.mult).then_inc(s2_read, 1)
                    yield
                    dve.wait_ge(s2_read, n + 1)
                    previous_step()
                    nc.vector.tensor_tensor(col(sc, A0), col(sc, SIG), col(sc, DOX), ALU.mult)
                    nc.vector.scalar_tensor_tensor(col(sc, A2), col(sc, U0), col(nu, NUM), col(sc, MU), ALU.mult, ALU.add)
                    step_done(nc.vector.tensor_tensor(col(sc, A1), col(sc, U0), col(sc, U0), ALU.mult))
                    yield
                    previous_step()
                    nc.vector.scalar_tensor_tensor(col(sc, A0), col(sc, A0), col(nu, NUV), col(sc, VAR), ALU.mult, ALU.add)
                    nc.vector.tensor_tensor(col(sc, A2), col(sc, A2), col(nu, BIAS_CD), ALU.add)
                    step_done(nc.vector.tensor_tensor(col(sc, A1), col(sc, DOO), col(sc, A1), ALU.subtract))
                    yield
                    previous_step()
                    step_done(nc.vector.scalar_tensor_tensor(col(sc, A0), col(sc, A1), col(nu, NUV2), col(sc, A0),
                                                             ALU.mult, ALU.add))
                    yield
                    previous_step()
                    nc.vector.tensor_scalar(col(sc, A0), col(sc, A0), 0.0, EPS, ALU.max, ALU.add).then_inc(var1_ready, 1)
                    for _ in range(ROOT_WAIT):
                        yield
                    dve.wait_ge(dev1_ready, n + 1)
                    dve.wait_ge(var1_ready, n + 1)
                    y, t = col(sc, A1), col(sc, ROOT2)
                    step_done(nc.vector.reciprocal(y, col(sc, ROOT)))
                    yield
                    previous_step()
                    step_done(nc.vector.tensor_tensor(t, y, y, ALU.mult))
                    yield
                    previous_step()
                    step_done(nc.vector.tensor_tensor(t, t, col(sc, A0), ALU.mult))
                    yield
                    previous_step()
                    step_done(nc.vector.tensor_scalar(t, t, -0.5, 1.5, ALU.mult, ALU.add))
                    yield
                    previous_step()
                    step_done(nc.vector.tensor_tensor(y, y, t, ALU.mult))
                    yield
                    previous_step()
                    step_done(nc.vector.tensor_scalar(col(sc, GS), y, G_UP, None, ALU.mult))
                    yield
                    previous_step()
                    nc.vector.scalar_tensor_tensor(col(sc, GB), col(sc, A2), -1.0, col(sc, GS), ALU.mult, ALU.mult)\
                        .then_inc(znorm_scalars, 1)

                def add_x(r):
                    dve.wait_ge(s_mm, 32 * n + 2 * r + 1)
                    part = img[k][:, 0, 2 * r:2 * r + 2, :].rearrange("p c w -> p (c w)")
                    nc.vector.scalar_tensor_tensor(part, bank[2 + 4 * (r % 2)][:, :], col(nu, ALPHA), part, ALU.mult, ALU.add)\
                        .then_inc(x1_up, 1)

                def rows_lo(r):
                    dve.wait_ge(t_hi, 16 * n + r + 1)
                    lo = trow[r % 2][64:P, :]
                    nc.vector.scalar_tensor_tensor(lo, bank[r % 2][64:P, :], T_DOWN, lo, ALU.mult, ALU.subtract).then_inc(t_lo, 1)

                rows_lo(0)
                rest = s2()
                for r in range(16):
                    next(rest, None)
                    if r < 15:
                        rows_lo(r + 1)
                    next(rest, None)
                    add_x(r)
                    conv_adds(2 + r)
                assert next(rest, "over") == "over"
                conv_adds(18)
                assert at[0] == STEPS, at[0]

            STEPS = DVE_STEPS
            setup()
            over_samples(dve, step)
            for u in range(9):
                conv_add(LAST, 1, u)


O_SCALE_INV = 2.0 ** -15
DVE_STEPS = 30


def _tables():
    import numpy as np
    p = np.arange(P)
    m = np.arange(M)

    def halves(a):
        hi = a.astype(np.float16)
        return hi, (a - hi).astype(np.float16)

    h = np.arange(2)[None, :, None] * P + p[:, None, None]
    ang = 2 * np.pi * (h * m % H) / H
    cf = np.concatenate([np.cos(ang), np.sin(ang)], -1).astype(np.float32)
    ang = 2 * np.pi * (h * m % W) / W
    lt = np.zeros((P, 4, 96), np.float32)
    for half in range(2):
        c, s = np.cos(ang[:, half]), np.sin(ang[:, half])
        lt[:, half, 0:32:2], lt[:, half, 1:32:2] = -s, c
        lt[:, 2 + half, 0:32:2], lt[:, 2 + half, 1:32:2] = -c, -s
    w = np.arange(W)
    ang = 2 * np.pi * (m[:, None] * w % W) / W
    hi, lo = halves(np.stack([np.cos(ang), np.sin(ang)], 1).reshape(32, W))
    cst = np.concatenate([hi, lo, hi, lo], 0)
    g, r, s = np.meshgrid(np.arange(4), np.arange(2), np.arange(4), indexing="ij")
    mm = (4 * g + s).reshape(32, 1)
    rr = r.reshape(32, 1)
    hh = np.arange(H)
    ang = 2 * np.pi * (mm * hh % H) / H
    e = np.where(rr == 0, np.cos(ang), -np.sin(ang))
    e[4] = 1.0
    hi, lo = halves(e * E_UP)
    et = np.concatenate([hi, lo, hi, lo], 0).reshape(P, 2, P)
    c = np.arange(C)
    same = (p[:, None] % C) // 2 == c // 2
    mask2 = np.repeat(same[:, :, None] / 512.0, 2, 2).astype(np.float32)
    sel = np.zeros((32, 2 * P), np.float32)
    sel[1, :P] = 1
    sel[:, P] = 1
    sel[0, P], sel[1, P] = 0, 2
    return {"cf": cf, "lt": lt, "cst": cst, "et": et, "ident": np.eye(P, dtype=np.float32),
            "rep": (p % C == c[:, None]).astype(np.float32), "mask2": mask2,
            "mg": same.astype(np.float32), "dw": (p[:, None] // C == np.arange(4)).astype(np.float32), "sel": sel}


_INS = ["x", "L0_conv_w_real", "L0_conv_w_imag", "L1_conv_weight", "L1_conv_bias"]


def kernel(**inputs):
    import numpy as _np
    import concourse.bacc as _bacc
    from concourse import mybir as _mybir
    from concourse.bass_utils import run_bass_kernel_spmd as _run

    nc = _bacc.Bacc("TRN2", target_bir_lowering=False, num_devices=1)
    arrays, args = {}, []
    for name, a in [(n, inputs[n]) for n in _INS] + list(_tables().items()):
        a = _np.ascontiguousarray(a)
        arrays[f"in_{name}_dram"] = a
        args.append(nc.dram_tensor(f"in_{name}_dram", a.shape, _mybir.dt.from_np(a.dtype), kind="ExternalInput").ap())
    o = nc.dram_tensor("out_0_dram", (B, C, H, W), _mybir.dt.float32, kind="ExternalOutput").ap()
    bass_spectral_then_conv(nc, *args, o)
    r = _run(nc, [arrays], core_ids=[0])
    return r.results[0]["out_0_dram"]
```

```python
import concourse.bass as bass
from concourse import mybir
from contextlib import ExitStack

B, C, H, W = 16, 32, 256, 256
N = H * W
M = 16
P = 128
EPS = 1e-5
K3 = 3
FFT = 512
CUT = (FFT - H) // 2
OUTW = H + K3 - 1 - CUT
NBLK = 33
COL0 = W - 4 * NBLK
TAPW = 4 + K3 - 1
X_UP = 4096.0
W_UP = 1024.0
O_DOWN = 2.0 ** -13
T_DOWN = 2.0 ** -4
E_UP = 1024.0
G_UP = 64.0
K_UP = 1024.0
O_SCALE_INV = 2.0 ** -15
DVE_STEPS = 30


def bass_spectral_then_conv(nc: bass.Bass, x, w_real, w_imag, conv_w, conv_b,
                            cf_d, l_d, cst_d, e_d, ident_d, rep_d, m2_d, mg_d, dw_d, sel_d, out, samples=B):
    f32, f16 = mybir.dt.float32, mybir.dt.float16
    ALU, ACT, AX = mybir.AluOpType, mybir.ActivationFunctionType, mybir.AxisListType
    ctx = ExitStack()
    with ctx:
        def sb(name, shape, dt):
            return ctx.enter_context(nc.sbuf_tensor(name, shape, dt))

        def sem(name):
            return ctx.enter_context(nc.semaphore(name))

        img = [sb(f"img{k}", [P, 2, C, W], f32) for k in range(2)]
        wmix = sb("wmix", [P, 2, 2, M, P], f16)
        colsum = sb("colsum", [P, 2, 512], f32)
        shared = sb("shared", [P, 2048], f32)
        turned = shared[:, :].rearrange("p (h m c) -> p h m c", h=2, m=32)
        obroad = shared[:, 0:1024].rearrange("p (k c f) -> p k c f", k=8, c=4)
        prod_oo = shared[0:32, 512:1024]
        ospec = shared[0:32, 1024:1536]
        prod_ox = shared[0:32, 1536:2048]
        trow = [shared[:, 256 * k:256 * k + 256].bitcast(f16) for k in range(2)]
        stats = sb("stats", [P, C, 6], f32)
        moments = sb("moments", [P, 2, C, 2], f32)
        meansq = sb("meansq", [P, C, 2], f32)
        xnorm = sb("xnorm", [P, 4, M, 2], f32)
        xtri = sb("xtri", [P, M, 2, 4, 3], f16)
        xdiag = sb("xdiag", [P, M * 2, 4, 12], f16)
        opair = sb("opair", [P, 2, 4, M, 2], f32)
        ostat = sb("ostat", [P, C, 32], f16)
        half = sb("half", [P, 3, 512], f32)
        edge = sb("edge", [2, 2, 9 * P], f32)
        gn = sb("gn", [P, 2, NBLK, OUTW], f16)
        prod_sum = sb("prod_sum", [32, 2, C], f32)
        junk = sb("junk", [P, 3 * C], f32)
        edge_out = sb("edge_out", [NBLK, 2, P], f32)
        wconv = sb("wconv", [P, 2, K3, TAPW * C], f16)
        bias_rows = sb("bias_rows", [P, C], f32)
        bias_half = sb("bias_half", [P, C], f16)
        cf = sb("cf", [P, 2, 32], f32)
        lt = sb("lt", [P, 4, 96], f32)
        cst = sb("cst", [P, W], f16)
        et = sb("et", [P, 2, P], f16)
        ident = sb("ident", [P, P], f32)
        ones = sb("ones", [P, P], f32)
        rep = sb("rep", [C, P], f32)
        mask2 = sb("mask2", [P, C, 2], f32)
        mask_g = sb("mask_g", [P, C], f32)
        dw_is = sb("dw_is", [P, 4], f32)
        sel = sb("sel", [32, 2 * P], f32)
        nu = sb("nu", [P, 12], f32)
        sc = sb("sc", [P, 32], f32)
        bank = [ctx.enter_context(nc.psum_tensor(f"bank{k}", [P, 512], f32)) for k in range(8)]

        wflat = gn[:, :, :, :].rearrange("p a b c -> p (a b c)").bitcast(f32)[:, 0:2 * 2048]\
            .rearrange("p (r f) -> p r f", r=2)
        conv_in, taps, wide = (half[:, :, :].rearrange("p a b -> p (a b)")[:, a:b] for a, b in
                               ((0, 288), (288, 576), (576, 576 + K3 * TAPW * C)))
        edge_rows = bank[2][:, 128:128 + 2 * NBLK]

        NU0, RNU0, NU1, RNU1, ALPHA, BETA, NUV, NUV2, NUM, BIAS_CD = range(10)
        MU, MS, MUSQ, VAR, VE, RS, XS, DC, DOX, DOO, U0, SIG, A0, A1, A2, GS, GB, ROOT, ROOT2 = range(19)

        def col(t, k, n=1):
            return t[:, k:k + n]

        tables_in = sem("tables_in")
        weights_in = sem("weights_in")
        slot_in = [sem(f"slot_in{s}") for s in range(4)]
        bias_in = sem("bias_in")
        ones_set = sem("ones_set")
        peak_col = sem("peak_col")
        peak_row = sem("peak_row")
        peak_got = sem("peak_got")
        peak_all = sem("peak_all")
        nu_set = sem("nu_set")
        conv_rep = sem("conv_rep")
        mix_hi = sem("mix_hi")
        wconv_set = sem("wconv_set")
        weights_done = sem("weights_done")
        cleared = sem("cleared")
        loaded = [[sem(f"loaded{k}{q}") for q in range(4)] for k in range(2)]
        cols_mm = sem("cols_mm")
        cols_sb = sem("cols_sb")
        turn_mm = sem("turn_mm")
        turn_sb = sem("turn_sb")
        moments_ready = sem("moments_ready")
        sums_mm = sem("sums_mm")
        var_ready = sem("var_ready")
        dev_ready = sem("dev_ready")
        var1_ready = sem("var1_ready")
        dev1_ready = sem("dev1_ready")
        spec_mm = sem("spec_mm")
        spec_read = sem("spec_read")
        xtri_ready = sem("xtri_ready")
        xdiag_ready = sem("xdiag_ready")
        mix_mm = sem("mix_mm")
        obroad_ready = sem("obroad_ready")
        oturn_mm = sem("oturn_mm")
        xturn_mm = sem("xturn_mm")
        ostat_hi = sem("ostat_hi")
        ostat_ready = sem("ostat_ready")
        ospec_ready = sem("ospec_ready")
        xt_read = sem("xt_read")
        prods_ready = sem("prods_ready")
        s2_mm = sem("s2_mm")
        s2_read = sem("s2_read")
        znorm_scalars = sem("znorm_scalars")
        t_mm = sem("t_mm")
        t_hi = sem("t_hi")
        t_lo = sem("t_lo")
        s_mm = sem("s_mm")
        x1_up = sem("x1_up")
        s_copied = sem("s_copied")
        x1_low = sem("x1_low")
        packed = sem("packed")
        corner_mm = sem("corner_mm")
        edge_turned = sem("edge_turned")
        z_ready = sem("z_ready")
        g_hi = sem("g_hi")
        g_lo = sem("g_lo")
        edge_mm = sem("edge_mm")
        edge_sb = sem("edge_sb")
        edge_back = [sem(f"edge_back{k}") for k in range(2)]
        edge_added = [sem(f"edge_added{k}") for k in range(2)]
        edge_done = sem("edge_done")
        edge_stored = sem("edge_stored")
        conv_mm = sem("conv_mm")
        conv_added = sem("conv_added")
        stored = [[sem(f"stored{t}{q}") for q in range(4)] for t in range(2)]
        tail_stored = sem("tail_stored")
        act_step = sem("act_step")
        dve_step = sem("dve_step")
        dve_setup = sem("dve_setup")

        PIECES = [(u, j) for u in range(9) for j in range(4 * u, min(4 * u + 5, NBLK))]
        SLOTS = [3, 0, 5, 4] + [5, 4, 4, 5, 3, 4, 4] + [0] * 9
        INV0 = 4
        S2_SLOT = INV0 + 5
        assert sum(SLOTS) == len(PIECES) == 41

        S2_WAIT, ROOT_WAIT, ROOT_STEP = 9, 3, 7

        def pieces_in(slot):
            return PIECES[sum(SLOTS[:slot]):sum(SLOTS[:slot + 1])]

        def banks_ending_in(slot):
            return [u for u, j in pieces_in(slot) if j == min(4 * u + 4, NBLK - 1)]

        def conv_ps(u):
            return bank[4 + u % 2]

        EDGE_J = [(0, 8), (8, 16), (16, 24), (24, NBLK)]
        CORNER = [(4 * k, min(4 * k + 4, NBLK)) for k in range(9)]

        QS = (3, 2, 1, 0)
        xr = x.rearrange("b (q c) (t p) w -> b t q p c w", q=4, t=2)
        outr = out.rearrange("b (q c) (t p) w -> b t q p c w", q=4, t=2)
        LOADS = (48, 32, 32, 32)
        LAST = samples - 1
        PAIRS = (samples - 2) // 2

        def over_samples(eng, step):
            step(0, 0, 0)
            if PAIRS:
                with eng.Fori(0, PAIRS) as p:
                    step(2 * p + 1, p, 1)
                    step(2 * p + 2, p + 1, 0)
            step(LAST, LAST // 2, 1)

        def xdiag_slot(s):
            rows = slice(32 * s, 32 * s + 32)
            return xdiag[rows, :, s, :], xtri[rows].rearrange("p n h g e -> p (n h) (g e)")

        def edge_chunk(k, q):
            w0, w1 = 4 * EDGE_J[q][0], min(4 * EDGE_J[q][1], OUTW)
            return img[k][0:2, 1, :, w0:w1], edge[0:2, q % 2, 0:C * (w1 - w0)].rearrange("p (w o) -> p o w", o=C)

        EDGE = 6
        TURNS = 10

        def group(s):
            return s if s < EDGE else s - 1

        def corner(s, part):
            if s != EDGE:
                j0, j1 = CORNER[group(s)]
                w = P * (j1 - j0)
                return half[:, s % 3, 0:w], w, gn[:, part, j0:j1, 2:OUTW]
            return half[:, s % 3, 0:2 * NBLK], 2 * NBLK, gn[:, part, :, 0:2]

        def corner_in(z, s):
            return z.rearrange("p (j h) -> p j h", h=P) if s != EDGE else z.rearrange("p (j r) -> p j r", r=2)

        block = ctx.enter_context(nc.Block())

        @block.sync
        def _(sp):
            for ri, w in enumerate((w_real, w_imag)):
                sp.dma_start(wflat[:, ri, :], w.rearrange("i (a o) m n -> (i a) (o m n)", a=4))\
                    .then_inc(weights_in, 16)
            sp.dma_start(conv_in[0:C].rearrange("c (o k) -> c o k", k=9),
                         conv_w.rearrange("o c a b -> c o (a b)")).then_inc(weights_in, 16)
            sp.dma_start(nu[0:C, BIAS_CD:BIAS_CD + 1], conv_b.rearrange("(c a) -> c a", a=1)).then_inc(weights_in, 16)
            for dst, src in ((cf, cf_d), (lt, l_d), (cst, cst_d), (et, e_d), (ident, ident_d), (rep, rep_d),
                             (mask2, m2_d), (mask_g, mg_d), (dw_is, dw_d), (sel, sel_d)):
                sp.dma_start(dst[:], src).then_inc(tables_in, 16)
            def fetch(b, k, t, q):
                dst, src = img[k][:, t, 8 * q:8 * q + 8, :], xr[b, t, q]
                if (t, q) == (0, 0):
                    sp.dma_start(dst[1:P], src[1:P]).then_inc(loaded[k][q], 16)
                    sp.dma_start(dst[0:1], src[0:1]).then_inc(loaded[k][q], 16)
                else:
                    sp.dma_start(dst, src).then_inc(loaded[k][q], 16)

            for q in QS:
                for t in range(2):
                    fetch(0, 0, t, q)
            for s in range(4):
                for ri, w in enumerate((w_real, w_imag)):
                    sp.dma_start(img[1][32 * s:32 * s + 32, ri].rearrange("p c w -> p (c w)"),
                                 w.rearrange("i o m n -> i (o m n)")).then_inc(slot_in[s], 16)
            sp.wait_ge(weights_done, 1)
            for q in QS:
                for t in range(2):
                    fetch(1, 1, t, q)

            def turn_over(n, k, load):
                def send(t, q, first=0):
                    sp.dma_start(outr[n - 1, t, q, first:P], img[1 - k][first:P, t, 8 * q:8 * q + 8, :])\
                        .then_inc(stored[t][q], 16)

                sp.wait_ge(x1_low, 16 * n)
                for q in QS:
                    send(1, q, OUTW - CUT)
                sp.wait_ge(edge_sb, n)
                for q, (j0, j1) in enumerate(EDGE_J):
                    if q >= 2:
                        sp.wait_ge(edge_added[q - 2], n)
                    for i in range(2):
                        sp.dma_start(edge[i:i + 1, q % 2, 0:P * (j1 - j0)].rearrange("p (j f) -> p j f", f=P),
                                     edge_out[j0:j1, i, :]).then_inc(edge_back[q % 2], 16)
                sp.wait_ge(edge_done, n)
                sp.dma_start(out[n - 1, :, CUT:OUTW, :].rearrange("c h w -> h c w"), img[1 - k][0:OUTW - CUT, 1])\
                    .then_inc(edge_stored, 16)
                if load:
                    for q in QS:
                        sp.wait_ge(stored[1][q], 16 * n)
                    sp.wait_ge(edge_stored, 16 * n)
                    for q in QS:
                        fetch(n + 1, 1 - k, 1, q)
                if isinstance(n, int) and n == samples:
                    sp.wait_ge(x1_up, 16 * n)
                    for w0, w1 in ((OUTW, W), (0, OUTW)):
                        if w0 == 0:
                            sp.wait_ge(conv_added, 9 * n)
                        for q in QS:
                            sp.dma_start(outr[n - 1, 0, q, :, :, w0:w1], img[1 - k][:, 0, 8 * q:8 * q + 8, w0:w1])\
                                .then_inc(tail_stored, 16)
                else:
                    sp.wait_ge(conv_added, 9 * n)
                    send(0, QS[0])
                    for i, q in enumerate(QS):
                        if i < 3:
                            send(0, QS[i + 1])
                        if load:
                            sp.wait_ge(stored[0][q], 16 * n)
                            fetch(n + 1, 1 - k, 0, q)

            if PAIRS:
                with sp.Fori(2, PAIRS + 2) as p:
                    turn_over(2 * p - 3, 1, True)
                    turn_over(2 * p - 2, 0, True)
            turn_over(LAST, 1, False)
            turn_over(samples, 0, False)
            for q in range(4):
                sp.wait_ge(stored[0][q], 16 * LAST)
                sp.wait_ge(stored[1][q], 16 * samples)
            sp.wait_ge(tail_stored, 128)
            sp.wait_ge(edge_stored, 16 * samples)

        @block.tensor
        def _(pe):
            def setup():
                pe.wait_ge(tables_in, 160)
                pe.wait_ge(peak_col, 2)
                nc.tensor.matmul(bank[0][0:1, 0:P], col(sc, 0), ident[:, :], start=True, stop=True)
                nc.tensor.matmul(bank[0][0:1, P:2 * P], col(sc, 1), ident[:, :], start=True, stop=True).then_inc(peak_row, 1)
                pe.wait_ge(ones_set, 1)
                pe.wait_ge(peak_got, 1)
                nc.tensor.matmul(bank[1][:, 0:2], ones[0:1, :], sc[0:1, 2:4], start=True, stop=True).then_inc(peak_all, 1)
                nc.tensor.matmul(bank[2][:, 0:288], rep[:, :], conv_in[0:C], start=True, stop=True)
                nc.tensor.matmul(bank[3][:, 0:1], rep[:, :], nu[0:C, BIAS_CD:BIAS_CD + 1], start=True, stop=True)\
                    .then_inc(conv_rep, 1)

            def conv_edge(n):
                pe.wait_ge(g_lo, TURNS * n + TURNS)
                for i in range(2):
                    pairs = [(OUTW - 1, 1), (OUTW - 2, 2)] if i == 0 else [(OUTW - 1, 2)]
                    terms = [(r, a, gh, wh) for r, a in pairs for gh, wh in ((0, 0), (0, 1), (1, 0))]
                    for k, (r, a, gh, wh) in enumerate(terms):
                        nc.tensor.matmul(bank[6][0:NBLK, i * P:i * P + 64], gn[:, gh, :, r],
                                         wconv[:, wh, a, 4 * C:6 * C], start=(k == 0), stop=False, skip_group_check=True)
                        last = nc.tensor.matmul(bank[6][0:NBLK - 1, i * P:i * P + P], gn[:, gh, 1:NBLK, r],
                                                wconv[:, wh, a, 0:4 * C], start=False, stop=(k == len(terms) - 1),
                                                skip_group_check=True)
                last.then_inc(edge_mm, 1)

            def conv_piece(n, u, j):
                if j == 0 or j >= 16 and j % 4 == 0:
                    pe.wait_ge(g_lo, TURNS * n + EDGE + 1 + max(0, j // 4 - EDGE + 1))
                if j == 4 * u and u >= 2:
                    pe.wait_ge(conv_added, 9 * n + u - 1)
                lo = 0 if j > 4 * u else 4
                hi = TAPW if j < 4 * u + 4 else 4
                at = (j - 1 - 4 * u + (1 if lo else 0)) * P
                jobs = [(a, gh, wh) for gh, wh in ((0, 0), (0, 1), (1, 0)) for a in range(K3)]
                ends = j == min(4 * u + 4, NBLK - 1)
                for k, (a, gh, wh) in enumerate(jobs):
                    last = nc.tensor.matmul(conv_ps(u)[:, at:at + (hi - lo) * C], gn[:, gh, j, 2 - a:2 - a + P],
                                            wconv[:, wh, a, lo * C:hi * C], start=(j == 4 * u and k == 0),
                                            stop=(ends and k == len(jobs) - 1), skip_group_check=True)
                if ends:
                    last.then_inc(conv_mm, 1)

            def corner_turn(n, s):
                v = group(s)
                if v == 0:
                    pe.wait_ge(x1_up, 16 * n + 16)
                    pe.wait_ge(s_copied, 16 * n + 16)
                if v >= 2:
                    pe.wait_ge(z_ready, TURNS * n + (s - 1 if s < EDGE or v == 8 else s - 2))
                pe.wait_ge(packed, 9 * n + v + 1)
                for j in range(CORNER[v][1] - CORNER[v][0]):
                    last = nc.tensor.transpose(bank[6 + v % 2][:, P * j:P * j + P], half[:, s % 3, P * j:P * j + P], ident[:, :])
                last.then_inc(corner_mm, 1)

            def edge_turn(n, k, i):
                for j in range(NBLK * i // 3, NBLK * (i + 1) // 3):
                    for d in range(4):
                        last = nc.tensor.matmul(edge_rows[32 * d:32 * d + 32, 2 * j:2 * j + 2],
                                                img[k][96:P, 0, :, COL0 + 4 * j + d], ident[96:P, P - 2:P],
                                                start=True, stop=True)
                last.then_inc(edge_turned, 1)

            def conv_slot(n, slot):
                for u, j in pieces_in(slot):
                    if (u, j) == (7, 28):
                        pe.wait_ge(s2_read, n + 2)
                    conv_piece(n, u, j)

            def step(n, use, k):
                prev = n - 1
                has_prev = not isinstance(n, int) or n > 0
                if has_prev:
                    pe.wait_ge(t_lo, 16 * n)
                for i, q in enumerate(QS):
                    pe.wait_ge(loaded[k][q], LOADS[q] * (use + 1))
                    if i > 0 or has_prev:
                        pe.wait_ge(cols_sb, 4 * n + i)
                    for t in range(2):
                        for j in range(4):
                            last = nc.tensor.matmul(
                                bank[0][32 * j:32 * j + 32, :], cf[:, t, :],
                                img[k][:, t, 8 * q + j:8 * q + j + 5:4, :], start=(t == 0), stop=(t == 1))
                    last.then_inc(cols_mm, 1)
                    if has_prev and 2 * i != EDGE:
                        corner_turn(prev, 2 * i)
                        edge_turn(prev, 1 - k, i)
                    pe.wait_ge(cols_sb, 4 * n + i + 1)
                    if i > 0 or has_prev:
                        pe.wait_ge(turn_sb, 4 * n + i)
                    else:
                        pe.wait_ge(nu_set, 1)
                    for e in range(2):
                        for h in range(2):
                            last = nc.tensor.transpose(bank[1][:, (h * 2 + e) * P:(h * 2 + e + 1) * P],
                                                       colsum[:, i % 2, e * W + h * P:e * W + h * P + P], ident[:, :])
                    last.then_inc(turn_mm, 1)
                    if has_prev and i < 3:
                        corner_turn(prev, 2 * i + 1)
                if has_prev:
                    corner_turn(prev, 7)
                    pe.wait_ge(z_ready, TURNS * prev + EDGE + 1)
                pe.wait_ge(moments_ready, n + 1)
                nc.tensor.matmul(bank[2][:, 0:P], ones[:, :], moments[:, :, :, :], start=True, stop=True).then_inc(sums_mm, 1)
                if has_prev:
                    corner_turn(prev, 8)
                pe.wait_ge(turn_sb, 4 * n + 4)
                for g in range(4):
                    for k4 in range(4):
                        ab, h = k4 // 2, k4 % 2
                        last = nc.tensor.matmul(bank[3][:, 32 * g:32 * g + 96],
                                                turned[:, h, 16 * ab + 4 * g:16 * ab + 4 * g + 4, :],
                                                lt[:, k4, :], start=(k4 == 0), stop=(k4 == 3))
                last.then_inc(spec_mm, 1)
                if has_prev:
                    corner_turn(prev, 9)
                    conv_slot(prev, 0)
                    conv_edge(prev)
                    conv_slot(prev, 1)
                pe.wait_ge(xdiag_ready, 4 * n + 4)
                if not has_prev:
                    pe.wait_ge(weights_done, 1)
                pe.wait_ge(spec_read, n + 1)
                for m in range(M):
                    terms = [(ri, wh, xh) for wh, xh in ((0, 0), (0, 1), (1, 0)) for ri in range(2)]
                    for t, (ri, wh, xh) in enumerate(terms):
                        rhs = xdiag[:, 2 * m + xh].rearrange("p s (g e) -> p (s g) e", e=3)[:, :, ri:ri + 2]
                        last = nc.tensor.matmul(bank[3][:, 32 * m:32 * m + 32], wmix[:, wh, ri, m, :], rhs,
                                                start=(t == 0), stop=(t == len(terms) - 1))
                last.then_inc(mix_mm, 1)
                if has_prev:
                    conv_slot(prev, 2)
                pe.wait_ge(obroad_ready, n + 1)
                for ri in range(2):
                    for s in range(4):
                        last = nc.tensor.transpose(bank[ri][:, P * s:P * s + P],
                                                   obroad[:, 4 * ri + s].rearrange("p c f -> p (c f)"), ident[:, :])
                    last.then_inc(oturn_mm, 1)
                for g in range(4):
                    last = nc.tensor.transpose(bank[7][0:32, P * g:P * g + P], xnorm[:, g], ident[:, :])
                last.then_inc(xturn_mm, 1)
                if has_prev:
                    conv_slot(prev, 3)
                pe.wait_ge(ostat_ready, n + 1)

                def over_w(r):
                    if r == 1:
                        pe.wait_ge(ospec_ready, n + 1)
                    for o in range(2):
                        for c in range(4):
                            last = nc.tensor.matmul(bank[r % 2][32 * c:32 * c + 32, o * W:o * W + W],
                                                    ostat[:, 2 * r + o, :], cst[:, :], start=True, stop=True)
                    last.then_inc(t_mm, 1)

                over_w(0)
                over_w(1)
                for r in range(16):
                    pe.wait_ge(t_lo, 16 * n + r + 1)
                    if r == 0 and has_prev:
                        pe.wait_ge(edge_sb, n)
                    for t in range(2):
                        if r >= 2:
                            pe.wait_ge((x1_up, s_copied)[t], 16 * n + r - 1)
                        if r == 1 and t == 1:
                            pe.wait_ge(xt_read, n + 1)
                        nc.tensor.matmul(bank[2 + 4 * (r % 2) + t][:, :], et[:, t, :], trow[r % 2], start=True, stop=True)\
                            .then_inc(s_mm, 1)
                    if r < 14:
                        over_w(r + 2)
                    if INV0 + r == S2_SLOT:
                        pe.wait_ge(prods_ready, n + 1)
                        if has_prev:
                            pe.wait_ge(conv_added, 9 * prev + 6)
                        nc.tensor.matmul(bank[5][:, 0:2 * C], ones[0:32, :], prod_sum[:, :, :], start=True, stop=True)
                        nc.tensor.matmul(bank[5][:, 2 * C:3 * C], sel[:, 0:P], ospec[:, 0:C], start=True, stop=True)\
                            .then_inc(s2_mm, 1)
                    if has_prev:
                        conv_slot(prev, INV0 + r)

            setup()
            over_samples(pe, step)
            pe.wait_ge(x1_up, 16 * samples)
            pe.wait_ge(s_copied, 16 * samples)
            for t in range(EDGE + 2):
                if t != EDGE:
                    corner_turn(LAST, t)
                if t < 3:
                    edge_turn(LAST, 1, t)
            pe.wait_ge(conv_added, 9 * LAST)
            for u, j in PIECES:
                if (u, j) in ((0, 2), (1, 4)):
                    corner_turn(LAST, EDGE + 2 + u)
                if (u, j) == (3, 12):
                    conv_edge(LAST)
                conv_piece(LAST, u, j)

        @block.scalar
        def _(act):
            def edge_out_copy(n):
                act.wait_ge(edge_mm, n + 1)
                src = bank[6][:, 0:2 * P].rearrange("p (i f) -> p i f", i=2)
                nc.scalar.activation(edge_out[0:32, :, :], src[0:32], ACT.Copy, scale=nu[0:32, BETA:BETA + 1])
                nc.scalar.activation(edge_out[32:33, :, 0:64], src[32:33, :, 0:64], ACT.Copy,
                                     scale=nu[32:33, BETA:BETA + 1]).then_inc(edge_sb, 1)

            def weights_hi():
                act.wait_ge(nu_set, 1)
                for s in range(4):
                    act.wait_ge(slot_in[s], 32)
                    rows = slice(32 * s, 32 * s + 32)
                    for ri in range(2):
                        src = img[1][rows, ri].rearrange("p c w -> p (c w)").rearrange("p (o g s n) -> p s n g o", o=C, g=4, s=4)[:, s]
                        dst = wmix[rows, 0, ri].rearrange("p n (g o) -> p n g o", g=4)
                        nc.scalar.activation(dst, src, ACT.Copy, scale=nu[rows, RNU0:RNU0 + 1]).then_inc(mix_hi, 1)

            def pack(n, k, s):
                if s == EDGE or s >= TURNS:
                    return
                if s == 0:
                    act.wait_ge(x1_low, 16 * n + 16)
                if s >= 3:
                    act.wait_ge(g_lo, TURNS * n + s - 2)
                j0, j1 = CORNER[group(s)]
                src = img[k][:, 1, :, COL0 + 4 * j0:COL0 + 4 * j1].rearrange("p c w -> p w c")
                nc.scalar.activation(half[:, s % 3, 0:P * (j1 - j0)].rearrange("p (w c) -> p w c", c=C), src, ACT.Copy)\
                    .then_inc(packed, 1)

            def normalise(n, k, s):
                if s == EDGE:
                    act.wait_ge(edge_turned, 3 * n + 3)
                    act.wait_ge(g_lo, TURNS * n + s - 2)
                else:
                    act.wait_ge(corner_mm, 9 * n + group(s) + 1)
                if s == 0:
                    act.wait_ge(znorm_scalars, n + 1)
                z, w, dst = corner(s, 0)
                src = bank[6 + group(s) % 2][:, 0:w] if s != EDGE else edge_rows
                nc.scalar.activation(z, src, ACT.Identity, bias=col(sc, GB), scale=col(sc, GS)).then_inc(z_ready, 1)
                act.wait_ge(z_ready, TURNS * n + s + 1)
                nc.scalar.activation(dst, corner_in(z, s), ACT.Copy).then_inc(g_hi, 1)
                pack(n, k, s + 2)

            def step(n, use, k):
                has_prev = not isinstance(n, int) or n > 0
                if has_prev:
                    pack(n - 1, 1 - k, 0)
                    pack(n - 1, 1 - k, 1)
                for i, q in enumerate(QS):
                    act.wait_ge(cols_mm, 4 * n + i + 1)
                    if i >= 2:
                        act.wait_ge(turn_mm, 4 * n + i - 1)
                    elif has_prev:
                        act.wait_ge(turn_mm, 4 * n)
                    nc.scalar.activation(colsum[:, i % 2, :], bank[0][:, :], ACT.Copy).then_inc(cols_sb, 1)
                    if has_prev:
                        normalise(n - 1, 1 - k, 2 * i)
                    act.wait_ge(turn_mm, 4 * n + i + 1)
                    dst = turned[:, :, :, 8 * q:8 * q + 8].rearrange("p h m c -> p h c m")
                    nc.scalar.activation(dst, bank[1][:, :].rearrange("p (h c m) -> p h c m", h=2, c=8),
                                         ACT.Copy).then_inc(turn_sb, 1)
                    if has_prev and i < 3:
                        normalise(n - 1, 1 - k, 2 * i + 1)
                if has_prev:
                    normalise(n - 1, 1 - k, 7)
                act.wait_ge(var_ready, n + 1)
                nc.scalar.activation(col(sc, ROOT), col(sc, VE), ACT.Sqrt).then_inc(dev_ready, 1)
                if has_prev:
                    normalise(n - 1, 1 - k, 8)
                    normalise(n - 1, 1 - k, 9)
                else:
                    weights_hi()
                if has_prev:
                    edge_out_copy(n - 1)
                act.wait_ge(mix_mm, n + 1)
                for g in range(4):
                    rows = slice(32 * g, 32 * g + 32)
                    src = bank[3][rows, :].rearrange("p (n s g e) -> p g s n e", n=M, s=4, g=4)[:, g]
                    nc.scalar.activation(opair[rows, 1], src, ACT.Copy).then_inc(act_step, 1)
                act.wait_ge(act_step, 6 * n + 4)
                pairs = opair[:, :, :, :, :].rearrange("p r s n e -> p r (s n) e")
                nc.scalar.activation(pairs[:, 0, :, 0], pairs[:, 1, :, 1], ACT.Copy).then_inc(act_step, 1)
                nc.scalar.activation(pairs[:, 0, :, 1], pairs[:, 1, :, 0], ACT.Copy, scale=-1.0).then_inc(act_step, 1)
                act.wait_ge(act_step, 6 * n + 6)
                src = opair[:, :, :, :, :].rearrange("p r s n e -> p (r s) (n e)").unsqueeze(2).broadcast_to([P, 8, 4, 32])
                nc.scalar.activation(obroad, src, ACT.Copy).then_inc(obroad_ready, 1)
                for ri in range(2):
                    act.wait_ge(oturn_mm, 2 * n + ri + 1)
                    dst = ostat[:, :, :].rearrange("p o (g r s) -> p r s g o", g=4, r=2)[:, ri]
                    nc.scalar.activation(dst, bank[ri][:, :].rearrange("p (s g o) -> p s g o", s=4, g=4),
                                         ACT.Copy, scale=O_DOWN).then_inc(ostat_hi, 1)
                nc.scalar.activation(ospec, bank[1][0:32, :], ACT.Copy).then_inc(ospec_ready, 1)
                def rows_hi(r):
                    act.wait_ge(t_mm, 16 * n + r + 1)
                    nc.scalar.activation(trow[r % 2], bank[r % 2][:, :], ACT.Copy, scale=T_DOWN).then_inc(t_hi, 1)

                rows_hi(0)
                for r in range(16):
                    if r < 15:
                        rows_hi(r + 1)
                    if r == 0 and not has_prev:
                        act.wait_ge(wconv_set, 1)
                    act.wait_ge(s_mm, 32 * n + 2 * r + 2)
                    if r >= 2:
                        act.wait_ge(x1_low, 16 * n + r - 1)
                    nc.scalar.activation(half[:, r % 2, :], bank[3 + 4 * (r % 2)][:, :], ACT.Copy,
                                         scale=col(nu, ALPHA)).then_inc(s_copied, 1)
                    if r == ROOT_STEP:
                        act.wait_ge(var1_ready, n + 1)
                        nc.scalar.activation(col(sc, ROOT), col(sc, A0), ACT.Sqrt).then_inc(dev1_ready, 1)
                if has_prev:
                    act.wait_ge(edge_done, n)

            over_samples(act, step)
            pack(LAST, 1, 0)
            pack(LAST, 1, 1)
            for t in range(TURNS):
                normalise(LAST, 1, t)
            edge_out_copy(LAST)

        @block.gpsimd
        def _(pool):
            nc.gpsimd.memset(xdiag[:, :, :, :], 0.0).then_inc(cleared, 1)
            nc.gpsimd.memset(edge_out[:, :, :], 0.0).then_inc(cleared, 1)
            nc.gpsimd.memset(bias_rows[:, :], 0.0).then_inc(cleared, 1)
            pool.wait_ge(cleared, 3)
            for c in range(4):
                pool.dma_start(bias_rows[32 * c:32 * c + 1, :], conv_b.rearrange("(a c) -> a c", a=1)).then_inc(bias_in, 16)

            def edge_add(n, k):
                for q in (2, 3):
                    pool.wait_ge(edge_back[q % 2], 64 * n + 64)
                    rows, src = edge_chunk(k, q)
                    last = nc.gpsimd.tensor_tensor(rows, rows, src, ALU.add)
                last.then_inc(edge_done, 1)

            def low_half(n, v):
                pool.wait_ge(g_hi, TURNS * n + v + 1)
                z, w, hi = corner(v, 0)
                nc.gpsimd.tensor_tensor(corner(v, 1)[2], corner_in(z, v), hi, ALU.subtract).then_inc(g_lo, 1)

            def step(n, use, k):
                if not isinstance(n, int) or n > 0:
                    for v in range(TURNS):
                        low_half(n - 1, v)
                    edge_add(n - 1, 1 - k)
                for r in range(16):
                    pool.wait_ge(s_copied, 16 * n + r + 1)
                    part = img[k][:, 1, 2 * r:2 * r + 2, :].rearrange("p c w -> p (c w)")
                    nc.gpsimd.tensor_tensor(part, part, half[:, r % 2, :], ALU.add).then_inc(x1_low, 1)

            over_samples(pool, step)
            for v in range(TURNS):
                low_half(LAST, v)
            edge_add(LAST, 1)

        @block.vector
        def _(dve):
            nc.vector.memset(ones[:, :], 1.0).then_inc(ones_set, 1)
            count = [0]

            def link(ins):
                count[0] += 1
                ins.then_inc(dve_setup, 1)
                dve.wait_ge(dve_setup, count[0])

            def setup():
                dve.wait_ge(weights_in, 64)
                nc.vector.tensor_reduce(col(sc, 4), wflat.rearrange("p r f -> p (r f)"), AX.X, ALU.max).then_inc(dve_setup, 1)
                nc.vector.tensor_reduce(col(sc, 5), wflat.rearrange("p r f -> p (r f)"), AX.X, ALU.min).then_inc(dve_setup, 1)
                nc.vector.memset(col(sc, 6, 4), 0.0).then_inc(dve_setup, 1)
                count[0] += 3
                dve.wait_ge(dve_setup, 3)
                link(nc.vector.tensor_reduce(sc[0:C, 6:7], conv_in[0:C], AX.X, ALU.max))
                link(nc.vector.tensor_reduce(sc[0:C, 7:8], conv_in[0:C], AX.X, ALU.min))
                link(nc.vector.tensor_reduce(sc[0:C, 8:9], nu[0:C, BIAS_CD:BIAS_CD + 1], AX.X, ALU.max))
                nc.vector.scalar_tensor_tensor(col(sc, 1), col(sc, 7), -1.0, col(sc, 6), ALU.mult, ALU.max).then_inc(peak_col, 1)
                link(nc.vector.scalar_tensor_tensor(col(sc, 5), col(sc, 5), -1.0, col(sc, 4), ALU.mult, ALU.max))
                link(nc.vector.scalar_tensor_tensor(col(sc, 9), col(sc, 8), -1.0, col(sc, 8), ALU.mult, ALU.max))
                nc.vector.scalar_tensor_tensor(col(sc, 0), col(sc, 9), 1.0 / 64, col(sc, 5), ALU.mult, ALU.max).then_inc(peak_col, 1)
                dve.wait_ge(peak_row, 1)
                nc.vector.tensor_reduce(sc[0:1, 2:4], bank[0][0:1, 0:2 * P].rearrange("p (k f) -> p k f", k=2), AX.X, ALU.max)\
                    .then_inc(peak_got, 1)
                dve.wait_ge(peak_all, 1)
                link(nc.vector.tensor_scalar(nu[:, NU0:NU0 + 3:2], bank[1][:, 0:2], 1e-30, None, ALU.max))
                link(nc.vector.reciprocal(col(sc, 6), col(nu, NU0)))
                link(nc.vector.reciprocal(col(sc, 7), col(nu, NU1)))
                link(nc.vector.tensor_scalar(col(nu, RNU0), col(sc, 6), W_UP, None, ALU.mult))
                link(nc.vector.tensor_scalar(col(nu, RNU1), col(sc, 7), K_UP, None, ALU.mult))
                nc.vector.tensor_scalar(col(nu, ALPHA), col(nu, NU0), O_SCALE_INV, None, ALU.mult)
                link(nc.vector.tensor_scalar(col(nu, BETA), col(nu, NU1), 1.0 / (FFT * G_UP * K_UP), None, ALU.mult))
                nc.vector.tensor_scalar(col(nu, NUV), col(nu, NU0), 2.0 ** -34, None, ALU.mult)
                link(nc.vector.tensor_scalar(col(nu, NUM), col(nu, NU0), 2.0 ** -23, None, ALU.mult))
                link(nc.vector.tensor_tensor(col(nu, NUV2), col(nu, NUM), col(nu, NUM), ALU.mult))
                dve.wait_ge(conv_rep, 1)
                dve.wait_ge(tables_in, 160)
                nc.vector.tensor_copy(col(nu, BIAS_CD), bank[3][:, 0:1]).then_inc(nu_set, 1)
                link(nc.vector.tensor_scalar(taps.rearrange("p (a b o) -> p a b o", a=3, b=3),
                                             bank[2][:, 0:288].rearrange("p (o a b) -> p a b o", a=3, b=3),
                                             col(nu, RNU1), None, ALU.mult))
                dve.wait_ge(cleared, 3)

            def setup_rest():
                wide3 = wide.rearrange("p (a f) -> p a f", a=3)
                taps3 = taps.rearrange("p (a f) -> p a f", a=3)
                for s in range(4):
                    rows = slice(32 * s, 32 * s + 32)
                    for ri in range(2):
                        dve.wait_ge(mix_hi, 2 * s + ri + 1)
                        for g in range(4):
                            src = img[1][rows, ri].rearrange("p c w -> p (c w)")\
                                .rearrange("p (o g s n) -> p g s n o", o=C, g=4, s=4)[:, g, s]
                            hi, lo = (wmix[rows, h, ri].rearrange("p n (g o) -> p g n o", g=4)[:, g] for h in range(2))
                            last = nc.vector.scalar_tensor_tensor(lo, src, nu[rows, RNU0:RNU0 + 1], hi, ALU.mult, ALU.subtract)
                last.then_inc(weights_done, 1)
                link(nc.vector.memset(wide3, 0.0))
                for d in range(4):
                    for a in range(K3):
                        part = wide3[:, a, d * C:(d + 3) * C]
                        link(nc.vector.scalar_tensor_tensor(part, taps3[:, a],
                                                            col(dw_is, d), part, ALU.mult, ALU.add))
                link(nc.vector.tensor_copy(wconv[:, 0], wide3))
                nc.vector.tensor_tensor(wconv[:, 1], wide3, wconv[:, 0], ALU.subtract).then_inc(wconv_set, 1)
                dve.wait_ge(bias_in, 64)
                link(nc.vector.tensor_scalar(bias_rows[:, :], bias_rows[:, :], col(nu, RNU0), 2.0 ** 9 / W_UP, ALU.mult, ALU.mult))
                link(nc.vector.tensor_copy(bias_half[:, :], bias_rows[:, :]))
                link(nc.vector.tensor_tensor(bias_half[64:P, :], bias_rows[64:P, :], bias_half[64:P, :], ALU.subtract))

            def conv_add(n, k, u):
                dve.wait_ge(conv_mm, 9 * n + u + 1)
                if u == 0:
                    dve.wait_ge(edge_turned, 3 * n + 3)
                w = min(16, OUTW - 16 * u)
                x1 = img[k][:, 0, :, 16 * u:16 * u + w]
                ps = conv_ps(u)[:, 0:w * C].rearrange("p (w o) -> p o w", o=C)
                nc.vector.scalar_tensor_tensor(x1, ps, col(nu, BETA), x1, ALU.mult, ALU.add).then_inc(conv_added, 1)

            def edge_add(n, k):
                dve.wait_ge(packed, 9 * n + 9)
                for q in (0, 1):
                    dve.wait_ge(edge_back[q % 2], 64 * n + 32)
                    rows, src = edge_chunk(k, q)
                    nc.vector.tensor_tensor(rows, rows, src, ALU.add).then_inc(edge_added[q], 1)

            def step(n, use, k):
                has_prev = not isinstance(n, int) or n > 0
                at = [0]

                def conv_adds(slot):
                    if has_prev:
                        for u in banks_ending_in(slot):
                            conv_add(n - 1, 1 - k, u)

                def then(ins):
                    at[0] += 1
                    ins.then_inc(dve_step, 1)
                    dve.wait_ge(dve_step, STEPS * n + at[0])

                def rsqrt(to, v, asked, root):
                    dve.wait_ge(asked, n + 1)
                    dve.wait_ge(root, n + 1)
                    then(nc.vector.reciprocal(col(sc, to), col(sc, ROOT)))
                    then(nc.vector.tensor_tensor(col(sc, ROOT2), col(sc, to), col(sc, to), ALU.mult))
                    then(nc.vector.tensor_tensor(col(sc, ROOT2), col(sc, ROOT2), col(sc, v), ALU.mult))
                    then(nc.vector.tensor_scalar(col(sc, ROOT2), col(sc, ROOT2), -0.5, 1.5, ALU.mult, ALU.add))
                    then(nc.vector.tensor_tensor(col(sc, to), col(sc, to), col(sc, ROOT2), ALU.mult))

                for i, q in enumerate(QS):
                    dve.wait_ge(loaded[k][q], LOADS[q] * (use + 1))
                    for c in range(8 * q, 8 * q + 8):
                        last = nc.vector.bn_stats(stats[:, c, :], img[k][:, :, c, :])
                then(last)
                mean, var = stats[:, :, 1:5:3], stats[:, :, 2:6:3]
                then(nc.vector.tensor_tensor(meansq[:, :, :], mean, mean, ALU.mult))
                if has_prev:
                    dve.wait_ge(sums_mm, n)
                nc.vector.tensor_copy(moments[:, 0], mean)
                nc.vector.scalar_tensor_tensor(moments[:, 1], var, 1.0 / 256, meansq[:, :, :], ALU.mult, ALU.add)\
                    .then_inc(moments_ready, 1)
                dve.wait_ge(moments_ready, n + 1)
                dve.wait_ge(sums_mm, n + 1)
                for kind, to in ((0, MU), (1, MS)):
                    then(nc.vector.tensor_tensor_reduce(
                        out=meansq[:, :, :].rearrange("p c e -> p (c e)"), in0=bank[2][:, 64 * kind:64 * kind + 64],
                        in1=mask2[:, :, :].rearrange("p c e -> p (c e)"), scale=1.0, scalar=0.0,
                        op0=ALU.mult, op1=ALU.add, accum_out=col(sc, to)))
                then(nc.vector.tensor_tensor(col(sc, MUSQ), col(sc, MU), col(sc, MU), ALU.mult))
                then(nc.vector.tensor_tensor(col(sc, VAR), col(sc, MS), col(sc, MUSQ), ALU.subtract))
                nc.vector.tensor_scalar(col(sc, VE), col(sc, VAR), 0.0, EPS, ALU.max, ALU.add).then_inc(var_ready, 1)
                rsqrt(RS, VE, var_ready, dev_ready)
                nc.vector.tensor_scalar(col(sc, XS), col(sc, RS), X_UP / N, None, ALU.mult)
                then(nc.vector.scalar_tensor_tensor(col(sc, DC), col(sc, MU), -X_UP, col(sc, RS), ALU.mult, ALU.mult))
                dve.wait_ge(spec_mm, n + 1)
                if has_prev:
                    dve.wait_ge(xturn_mm, n)
                nc.vector.tensor_scalar(xnorm[:, :, :, :].rearrange("p g n e -> p (g n e)"), bank[3][:, 0:P],
                                        col(sc, XS), None, ALU.mult).then_inc(spec_read, 1)
                dve.wait_ge(spec_read, n + 1)
                then(nc.vector.tensor_tensor(xnorm[0:32, 0, 0, 1:2], xnorm[0:32, 0, 0, 1:2], sc[0:32, DC:DC + 1], ALU.add))
                xn = xnorm[:, :, :, :].rearrange("p g n e -> p n g e")
                then(nc.vector.tensor_copy(xtri[:, :, 0, :, 0:2], xn))
                then(nc.vector.tensor_tensor(xtri[:, :, 1, :, 0:2], xn, xtri[:, :, 0, :, 0:2], ALU.subtract))
                tri = xtri[:, :, :, :, :].rearrange("p n h g e -> p (n h g) e")
                nc.vector.tensor_scalar(tri[:, :, 2], tri[:, :, 0], -1.0, None, ALU.mult).then_inc(xtri_ready, 1)
                dve.wait_ge(xtri_ready, n + 1)
                if has_prev:
                    dve.wait_ge(mix_mm, n)
                for s in range(4):
                    nc.vector.tensor_copy(*xdiag_slot(s)).then_inc(xdiag_ready, 1)
                if not has_prev:
                    setup_rest()
                conv_adds(0)
                conv_adds(1)
                if has_prev:
                    edge_add(n - 1, 1 - k)
                conv_adds(2)
                for ri in range(2):
                    dve.wait_ge(ostat_hi, 2 * n + ri + 1)
                    for s in range(4):
                        lo = ostat[64:P, :, :].rearrange("p o (g r s) -> p r s g o", g=4, r=2)[:, ri, s]
                        src = bank[ri][64:P, P * s:P * s + P].rearrange("p (g o) -> p g o", g=4)
                        last = nc.vector.scalar_tensor_tensor(lo, src, O_DOWN, lo, ALU.mult, ALU.subtract)
                then(last)
                nc.vector.tensor_copy(ostat[:, :, 4], bias_half[:, :]).then_inc(ostat_ready, 1)
                dve.wait_ge(xturn_mm, n + 1)
                dve.wait_ge(ospec_ready, n + 1)
                xt = bank[7][0:32, :].rearrange("p (g s c) -> p s g c", g=4, s=4)
                for s in range(4):
                    last = nc.vector.tensor_tensor(prod_ox[:, P * s:P * s + P].rearrange("p (g c) -> p g c", g=4), xt[:, s],
                                                   ospec[:, P * s:P * s + P].rearrange("p (g c) -> p g c", g=4), ALU.mult)
                last.then_inc(xt_read, 1)

                def s2():
                    def step_done(ins):
                        at[0] += 1
                        ins.then_inc(dve_step, 1)

                    def previous_step():
                        dve.wait_ge(dve_step, STEPS * n + at[0])

                    step_done(nc.vector.tensor_tensor(prod_oo, ospec, ospec, ALU.mult))
                    yield
                    previous_step()
                    step_done(nc.vector.tensor_scalar(prod_oo[:, 0:C], prod_oo[:, 0:C], sel[:, P:P + 1], None, ALU.mult))
                    dve.wait_ge(xt_read, n + 1)
                    nc.vector.tensor_reduce(prod_sum[:, 0, :], prod_ox.rearrange("p (k c) -> p c k", c=C), AX.X, ALU.add)
                    yield
                    previous_step()
                    nc.vector.tensor_reduce(prod_sum[:, 1, :], prod_oo.rearrange("p (k c) -> p c k", c=C), AX.X, ALU.add)\
                        .then_inc(prods_ready, 1)
                    for _ in range(S2_WAIT):
                        yield
                    dve.wait_ge(s2_mm, n + 1)
                    for i, to in enumerate((DOX, DOO, U0)):
                        step_done(nc.vector.tensor_tensor_reduce(
                            out=junk[:, i * C:i * C + C], in0=bank[5][:, C * i:C * i + C], in1=mask_g[:, :],
                            scale=1.0, scalar=0.0, op0=ALU.mult, op1=ALU.add, accum_out=col(sc, to)))
                    nc.vector.tensor_tensor(col(sc, SIG), col(sc, VE), col(sc, RS), ALU.mult).then_inc(s2_read, 1)
                    yield
                    dve.wait_ge(s2_read, n + 1)
                    previous_step()
                    nc.vector.tensor_tensor(col(sc, A0), col(sc, SIG), col(sc, DOX), ALU.mult)
                    nc.vector.scalar_tensor_tensor(col(sc, A2), col(sc, U0), col(nu, NUM), col(sc, MU), ALU.mult, ALU.add)
                    step_done(nc.vector.tensor_tensor(col(sc, A1), col(sc, U0), col(sc, U0), ALU.mult))
                    yield
                    previous_step()
                    nc.vector.scalar_tensor_tensor(col(sc, A0), col(sc, A0), col(nu, NUV), col(sc, VAR), ALU.mult, ALU.add)
                    nc.vector.tensor_tensor(col(sc, A2), col(sc, A2), col(nu, BIAS_CD), ALU.add)
                    step_done(nc.vector.tensor_tensor(col(sc, A1), col(sc, DOO), col(sc, A1), ALU.subtract))
                    yield
                    previous_step()
                    step_done(nc.vector.scalar_tensor_tensor(col(sc, A0), col(sc, A1), col(nu, NUV2), col(sc, A0),
                                                             ALU.mult, ALU.add))
                    yield
                    previous_step()
                    nc.vector.tensor_scalar(col(sc, A0), col(sc, A0), 0.0, EPS, ALU.max, ALU.add).then_inc(var1_ready, 1)
                    for _ in range(ROOT_WAIT):
                        yield
                    dve.wait_ge(dev1_ready, n + 1)
                    dve.wait_ge(var1_ready, n + 1)
                    y, t = col(sc, A1), col(sc, ROOT2)
                    step_done(nc.vector.reciprocal(y, col(sc, ROOT)))
                    yield
                    previous_step()
                    step_done(nc.vector.tensor_tensor(t, y, y, ALU.mult))
                    yield
                    previous_step()
                    step_done(nc.vector.tensor_tensor(t, t, col(sc, A0), ALU.mult))
                    yield
                    previous_step()
                    step_done(nc.vector.tensor_scalar(t, t, -0.5, 1.5, ALU.mult, ALU.add))
                    yield
                    previous_step()
                    step_done(nc.vector.tensor_tensor(y, y, t, ALU.mult))
                    yield
                    previous_step()
                    step_done(nc.vector.tensor_scalar(col(sc, GS), y, G_UP, None, ALU.mult))
                    yield
                    previous_step()
                    nc.vector.scalar_tensor_tensor(col(sc, GB), col(sc, A2), -1.0, col(sc, GS), ALU.mult, ALU.mult)\
                        .then_inc(znorm_scalars, 1)

                def add_x(r):
                    dve.wait_ge(s_mm, 32 * n + 2 * r + 1)
                    part = img[k][:, 0, 2 * r:2 * r + 2, :].rearrange("p c w -> p (c w)")
                    nc.vector.scalar_tensor_tensor(part, bank[2 + 4 * (r % 2)][:, :], col(nu, ALPHA), part, ALU.mult, ALU.add)\
                        .then_inc(x1_up, 1)

                def rows_lo(r):
                    dve.wait_ge(t_hi, 16 * n + r + 1)
                    lo = trow[r % 2][64:P, :]
                    nc.vector.scalar_tensor_tensor(lo, bank[r % 2][64:P, :], T_DOWN, lo, ALU.mult, ALU.subtract).then_inc(t_lo, 1)

                rows_lo(0)
                rest = s2()
                for r in range(16):
                    next(rest, None)
                    if r < 15:
                        rows_lo(r + 1)
                    next(rest, None)
                    add_x(r)
                    conv_adds(INV0 - 1 + r)
                assert next(rest, "over") == "over"
                conv_adds(INV0 + 15)
                assert at[0] == STEPS, at[0]

            STEPS = DVE_STEPS
            setup()
            over_samples(dve, step)
            for u in range(9):
                conv_add(LAST, 1, u)
                if u == 3:
                    edge_add(LAST, 1)


def _tables():
    import numpy as np
    p = np.arange(P)
    m = np.arange(M)

    def halves(a):
        hi = a.astype(np.float16)
        return hi, (a - hi).astype(np.float16)

    h = np.arange(2)[None, :, None] * P + p[:, None, None]
    ang = 2 * np.pi * (h * m % H) / H
    cf = np.concatenate([np.cos(ang), np.sin(ang)], -1).astype(np.float32)
    ang = 2 * np.pi * (h * m % W) / W
    lt = np.zeros((P, 4, 96), np.float32)
    for half in range(2):
        c, s = np.cos(ang[:, half]), np.sin(ang[:, half])
        lt[:, half, 0:32:2], lt[:, half, 1:32:2] = -s, c
        lt[:, 2 + half, 0:32:2], lt[:, 2 + half, 1:32:2] = -c, -s
    w = np.arange(W)
    ang = 2 * np.pi * (m[:, None] * w % W) / W
    hi, lo = halves(np.stack([np.cos(ang), np.sin(ang)], 1).reshape(32, W))
    cst = np.concatenate([hi, lo, hi, lo], 0)
    g, r, s = np.meshgrid(np.arange(4), np.arange(2), np.arange(4), indexing="ij")
    mm = (4 * g + s).reshape(32, 1)
    rr = r.reshape(32, 1)
    hh = np.arange(H)
    ang = 2 * np.pi * (mm * hh % H) / H
    e = np.where(rr == 0, np.cos(ang), -np.sin(ang))
    e[4] = 1.0
    hi, lo = halves(e * E_UP)
    et = np.concatenate([hi, lo, hi, lo], 0).reshape(P, 2, P)
    c = np.arange(C)
    same = (p[:, None] % C) // 2 == c // 2
    mask2 = np.repeat(same[:, :, None] / 512.0, 2, 2).astype(np.float32)
    sel = np.zeros((32, 2 * P), np.float32)
    sel[1, :P] = 1
    sel[:, P] = 1
    sel[0, P], sel[1, P] = 0, 2
    return {"cf": cf, "lt": lt, "cst": cst, "et": et, "ident": np.eye(P, dtype=np.float32),
            "rep": (p % C == c[:, None]).astype(np.float32), "mask2": mask2,
            "mg": same.astype(np.float32), "dw": (p[:, None] // C == np.arange(4)).astype(np.float32), "sel": sel}


_INS = ["x", "L0_conv_w_real", "L0_conv_w_imag", "L1_conv_weight", "L1_conv_bias"]


def kernel(**inputs):
    import numpy as _np
    import concourse.bacc as _bacc
    from concourse import mybir as _mybir
    from concourse.bass_utils import run_bass_kernel_spmd as _run

    nc = _bacc.Bacc("TRN2", target_bir_lowering=False, num_devices=1)
    arrays, args = {}, []
    for name, a in [(n, inputs[n]) for n in _INS] + list(_tables().items()):
        a = _np.ascontiguousarray(a)
        arrays[f"in_{name}_dram"] = a
        args.append(nc.dram_tensor(f"in_{name}_dram", a.shape, _mybir.dt.from_np(a.dtype), kind="ExternalInput").ap())
    o = nc.dram_tensor("out_0_dram", (B, C, H, W), _mybir.dt.float32, kind="ExternalOutput").ap()
    bass_spectral_then_conv(nc, *args, o)
    r = _run(nc, [arrays], core_ids=[0])
    return r.results[0]["out_0_dram"]
```
